# Optimizing a Trainium2 kernel written in Bass

```python
import numpy as np
import jax
import jax.numpy as jnp

def _softmax(x, axis=-1):
    return jax.nn.softmax(x, axis=axis)

def _gelu(x):
    return jax.nn.gelu(x, approximate=True)

def _silu(x):
    return jax.nn.silu(x)

def _sigmoid(x):
    return jax.nn.sigmoid(x)

def _layernorm(x, axis=-1, eps=1e-05):
    m = jnp.mean(x, axis=axis, keepdims=True)
    v = jnp.var(x, axis=axis, keepdims=True)
    return (x - m) / jnp.sqrt(v + eps)

def _scatter_add(tgt, idx, src, axis=0):
    return tgt.at[idx].add(src)

def _segment_sum(src, seg, n):
    return jax.ops.segment_sum(src, seg, n)
kernel_name = 'mk_cond_seq_d1_seqx_r2_4bd396'

def setup_inputs(seed: int=0):
    np.random.seed(seed)
    _w = jnp.asarray

    def _rec_inputs():
        import jax
        import jax.numpy as jnp
        _rk = jax.random.key(seed)
        x = -0.0002928 + 1 * jax.random.normal(jax.random.fold_in(_rk, 1), (8, 1024, 512), jnp.float32)
        _lenS = 1024 - jax.random.randint(jax.random.fold_in(_rk, 7), (8,), 0, max(1, 1024 // 4) + 1, jnp.int32)
        _lenS2 = 1024 - jax.random.randint(jax.random.fold_in(_rk, 8), (8,), 0, max(1, 1024 // 4) + 1, jnp.int32)
        cond_1024 = 0.0061147 + 1.02565 * jax.random.normal(jax.random.fold_in(_rk, 11), (8, 512), jnp.float32)
        return (x, cond_1024)
    x, cond_1024 = _rec_inputs()

    def _L0_cond_setup():
        import jax, jax.numpy as jnp
        import numpy as np
        D = 512
        H = 16
        HD = 4 * D
        B, T = (4, 512)
        EPS = 1e-05

        def _layernorm(x, g, b):
            mu = jnp.mean(x, axis=-1, keepdims=True)
            var = jnp.mean(jnp.square(x - mu), axis=-1, keepdims=True)
            return (x - mu) * jax.lax.rsqrt(var + EPS) * g + b

        def _attention(x, Wqkv, Wproj, bproj):
            b, t, c = x.shape
            hd = c // H
            qkv = (x @ Wqkv).reshape(b, t, 3, H, hd).transpose(2, 0, 3, 1, 4)
            q, k, v = (qkv[0], qkv[1], qkv[2])
            scale = hd ** (-0.5)
            scores = jnp.einsum('bhqd,bhkd->bhqk', q, k) * scale
            causal = jnp.tril(jnp.ones((t, t), bool))
            scores = jnp.where(causal, scores, -jnp.inf)
            attn = jax.nn.softmax(scores, axis=-1)
            out = jnp.einsum('bhqk,bhkd->bhqd', attn, v)
            out = out.transpose(0, 2, 1, 3).reshape(b, t, c)
            return out @ Wproj + bproj
        key = jax.random.key(seed)
        ks = jax.random.split(key, 12)
        s = 0.02
        return {'x': jax.random.normal(ks[0], (B, T, D), jnp.float32), 'condition': jax.random.normal(ks[1], (B, D), jnp.float32), 'Wqkv': jax.random.normal(ks[2], (D, 3 * D), jnp.float32) * s, 'Wproj': jax.random.normal(ks[3], (D, D), jnp.float32) * s, 'bproj': jnp.zeros((D,), jnp.float32), 'W1': jax.random.normal(ks[4], (D, HD), jnp.float32) * s, 'b1': jnp.zeros((HD,), jnp.float32), 'W2': jax.random.normal(ks[5], (HD, D), jnp.float32) * s, 'b2': jnp.zeros((D,), jnp.float32), 'g1': jnp.ones((D,), jnp.float32), 'be1': jnp.zeros((D,), jnp.float32), 'g2': jnp.ones((D,), jnp.float32), 'be2': jnp.zeros((D,), jnp.float32), 'Wada': jax.random.normal(ks[6], (D, 6 * D), jnp.float32) * s, 'bada': jax.random.normal(ks[7], (6 * D,), jnp.float32) * s}
    _L0_cond_all = _L0_cond_setup()
    _L0_cond_in = {k: v for k, v in _L0_cond_all.items() if k in ('Wqkv', 'Wproj', 'bproj', 'W1', 'b1', 'W2', 'b2', 'g1', 'be1', 'g2', 'be2', 'Wada', 'bada')}
    del _L0_cond_all
    return {'x': x, 'cond_1024': cond_1024, 'L0_cond_Wqkv': _L0_cond_in['Wqkv'], 'L0_cond_Wproj': _L0_cond_in['Wproj'], 'L0_cond_bproj': _L0_cond_in['bproj'], 'L0_cond_W1': _L0_cond_in['W1'], 'L0_cond_b1': _L0_cond_in['b1'], 'L0_cond_W2': _L0_cond_in['W2'], 'L0_cond_b2': _L0_cond_in['b2'], 'L0_cond_g1': _L0_cond_in['g1'], 'L0_cond_be1': _L0_cond_in['be1'], 'L0_cond_g2': _L0_cond_in['g2'], 'L0_cond_be2': _L0_cond_in['be2'], 'L0_cond_Wada': _L0_cond_in['Wada'], 'L0_cond_bada': _L0_cond_in['bada']}

def reference(x, cond_1024, L0_cond_Wqkv, L0_cond_Wproj, L0_cond_bproj, L0_cond_W1, L0_cond_b1, L0_cond_W2, L0_cond_b2, L0_cond_g1, L0_cond_be1, L0_cond_g2, L0_cond_be2, L0_cond_Wada, L0_cond_bada):
    import jax
    import jax.numpy as jnp

    def _L0_cond_ref(x, condition, Wqkv, Wproj, bproj, W1, b1, W2, b2, g1, be1, g2, be2, Wada, bada):
        import jax, jax.numpy as jnp
        import numpy as np
        D = 512
        H = 16
        HD = 4 * D
        B, T = (4, 512)
        EPS = 1e-05

        def _layernorm(x, g, b):
            mu = jnp.mean(x, axis=-1, keepdims=True)
            var = jnp.mean(jnp.square(x - mu), axis=-1, keepdims=True)
            return (x - mu) * jax.lax.rsqrt(var + EPS) * g + b

        def _attention(x, Wqkv, Wproj, bproj):
            b, t, c = x.shape
            hd = c // H
            qkv = (x @ Wqkv).reshape(b, t, 3, H, hd).transpose(2, 0, 3, 1, 4)
            q, k, v = (qkv[0], qkv[1], qkv[2])
            scale = hd ** (-0.5)
            scores = jnp.einsum('bhqd,bhkd->bhqk', q, k) * scale
            causal = jnp.tril(jnp.ones((t, t), bool))
            scores = jnp.where(causal, scores, -jnp.inf)
            attn = jax.nn.softmax(scores, axis=-1)
            out = jnp.einsum('bhqk,bhkd->bhqd', attn, v)
            out = out.transpose(0, 2, 1, 3).reshape(b, t, c)
            return out @ Wproj + bproj
        mod = jax.nn.silu(condition) @ Wada + bada
        sh_a, sc_a, gt_a, sh_m, sc_m, gt_m = jnp.split(mod, 6, axis=1)
        xn = _layernorm(x, g1, be1)
        xm = xn * (1.0 + sc_a[:, None, :]) + sh_a[:, None, :]
        x = x + gt_a[:, None, :] * _attention(xm, Wqkv, Wproj, bproj)
        xn = _layernorm(x, g2, be2)
        xm = xn * (1.0 + sc_m[:, None, :]) + sh_m[:, None, :]
        h = jax.nn.gelu(xm @ W1 + b1, approximate=False)
        x = x + gt_m[:, None, :] * (h @ W2 + b2)
        return x
    x = _L0_cond_ref(x, cond_1024, L0_cond_Wqkv, L0_cond_Wproj, L0_cond_bproj, L0_cond_W1, L0_cond_b1, L0_cond_W2, L0_cond_b2, L0_cond_g1, L0_cond_be1, L0_cond_g2, L0_cond_be2, L0_cond_Wada, L0_cond_bada)
    return x

_drawn_inputs = setup_inputs


def setup_inputs(seed=0):
    import zlib

    import numpy as np

    out = dict(_drawn_inputs(seed))
    spreads = {'L0_cond_bproj': (0.0, 0.281),
     'L0_cond_b1': (0.0, 0.533),
     'L0_cond_b2': (0.0, 0.32),
     'L0_cond_g1': (1.0, 0.6),
     'L0_cond_be1': (0.0, 0.8),
     'L0_cond_g2': (1.0, 0.6),
     'L0_cond_be2': (0.0, 0.8)}
    factors = {'L0_cond_Wqkv': 3.113, 'L0_cond_Wproj': 3.082, 'L0_cond_bada': 8.0}
    for name, (base, spread) in spreads.items():
        noise = np.random.default_rng([zlib.crc32(name.encode()), seed]).standard_normal(out[name].shape)
        drawn = base * np.exp(spread * noise) if base else spread * noise
        out[name] = jnp.asarray(drawn.astype(out[name].dtype))
    for name, factor in factors.items():
        out[name] = (out[name] * factor).astype(out[name].dtype)
    return out
```

```python
from contextlib import ExitStack

import concourse.bass as bass
from concourse import mybir

ALU = mybir.AluOpType
ACT = mybir.ActivationFunctionType
AX_X = mybir.AxisListType.X
F32 = mybir.dt.float32
F32R = mybir.dt.float32r
BF16 = mybir.dt.bfloat16

P = 128
EPS = 1e-5
MASKED = -1e30
LOWEST = -3e38

GH = 4
RA = 256
AHEAD = 5
HALF = 512
NSTEP = 12
RING = 6
LAG = 4
LOW_LAG = 2


def score_chunks():
    out = []
    for half in range(2):
        for kt in range(4 * (half + 1)):
            q0 = max(HALF * half, P * kt)
            out.append((half, kt, q0, HALF * (half + 1) - q0))
    return out


def max_chunks():
    out = []
    for qt in range(8):
        for part in range(1 + qt // 4):
            k0 = HALF * part
            out.append((qt, part, k0, min(HALF, P * (qt + 1) - k0)))
    return out


CHUNKS = score_chunks()
MAXES = max_chunks()
NMAX = len(MAXES) + 1
assert len(CHUNKS) == NSTEP

MAX_AT = {c: [2 * c, 2 * c + 1] for c in range(6)} | {7: [12]}
LN_STATS_AT, LN_TURN_AT, LN_SPLIT_AT = 6, 8, 9
A_ITEMS = ["v0", "v1"] + [f"qk{m}" for m in range(8)]
A_AT = dict(zip([11, 18, 20, 22, 30, 32, 34, 42, 44, 46], A_ITEMS))
A_NTURN, A_NITEM = 2, len(A_ITEMS)
A_N = A_NTURN + A_NITEM


def wait(eng, sem, value):
    if isinstance(value, int) and value <= 0:
        return
    eng.wait_ge(sem, value)


def build(nc, x, cond, Wqkv, Wproj, bproj, W1, b1, W2, b2, g1, be1, g2, be2, Wada, bada, out):
    B, T, D = x.shape
    H, HD = 16, 32
    F = W1.shape[1]
    KT = D // P
    FT = F // P
    ROWS = B * T
    QK3 = 3 * D
    SCALE = float(HD) ** -0.5
    VW = 2 * HD + 1
    NIT = B * H // GH
    NA = ROWS // RA
    NR = RA // P
    IPB = H // GH
    assert NIT == NA == 32 and KT == 4 and NR == 2 and T == 1024 and IPB == 4

    x_rows = x.rearrange("b t d -> (b t) d")
    out_rows = out.rearrange("b t d -> (b t) d")
    qk_dram = nc.dram_tensor("qk_split", (2, IPB, 2, P, ROWS), F32, kind="Internal").ap()
    v_dram = nc.dram_tensor("v_split", (ROWS, H, VW), F32, kind="Internal").ap()
    o_dram = nc.dram_tensor("attended", (H, VW, ROWS), F32, kind="Internal").ap()
    mod_dram = nc.dram_tensor("modulation", (6, B, D), F32, kind="Internal").ap()

    with ExitStack() as keep:
        sems = {}

        def sem(name):
            if name not in sems:
                sems[name] = keep.enter_context(nc.semaphore(name))
            return sems[name]

        def sb(stack, name, shape, dt=F32):
            return stack.enter_context(nc.sbuf_tensor(name, shape, dt))

        def psum(stack, name, shape):
            return stack.enter_context(nc.psum_tensor(name, shape, F32))

        ident = sb(keep, "ident", [P, P])
        coef = sb(keep, "coef", [P, 4, B, KT])
        b1c = sb(keep, "b1c", [P, FT])
        gb = sb(keep, "gb", [P, 4, KT])

        power = sb(keep, "power", [P, NR])

        att = ExitStack()
        ident_b = sb(att, "ident_b", [P, P], BF16)
        mask_q = sb(att, "mask_q", [P, P], BF16)
        mask_k = sb(att, "mask_k", [P, P], BF16)
        wqkv_h = sb(att, "wqkv_h", [P, KT, QK3], F32R)
        wqkv_l = sb(att, "wqkv_l", [P, KT, QK3], F32R)
        wraw = sb(att, "wraw", [P, 2, QK3])
        wada = sb(att, "wada", [P, 2, KT, D])
        bada_sb = sb(att, "bada_sb", [B, 2, D])
        mod = sb(att, "mod", [B, 2, D])
        csb = sb(att, "csb", [B, 4, D])
        sT = sb(att, "sT", [P, KT, B])
        xin = sb(att, "xin", [P, NR, D])
        xn = sb(att, "xn", [P, NR, D])
        yT = sb(att, "yT", [P, KT, RA])
        xm_h = sb(att, "xm_h", [P, KT, RA], F32R)
        xm_l = sb(att, "xm_l", [P, KT, RA], F32R)
        stats = sb(att, "stats", [P, NR, 6])
        aggr = sb(att, "aggr", [P, NR, 2])
        rstd = sb(att, "rstd", [P, NR])
        veps = sb(att, "veps", [P, NR])
        qk_h = sb(att, "qk_h", [P, 2, RA], F32R)
        qk_l = sb(att, "qk_l", [P, 2, RA], F32R)
        vaug = sb(att, "vaug", [P, NR, H, VW], F32R)
        qst = sb(att, "qst", [P, GH, T], F32R)
        kst = sb(att, "kst", [P, GH, T], F32R)
        vst = sb(att, "vst", [P, GH, T // P, VW], F32R)
        e_f = sb(att, "e_f", [P, RING, HALF])
        e_h = sb(att, "e_h", [P, RING, HALF], F32R)
        e_l = sb(att, "e_l", [P, RING, HALF], F32R)
        o_sb = sb(att, "o_sb", [VW, 2, HALF])
        mx = sb(att, "mx", [P, 2, 8])
        mxc = sb(att, "mxc", [P, 8])
        m_row = sb(att, "m_row", [8, 2, P], F32R)
        psS = psum(att, "psS", [P, 2, HALF])
        psT = psum(att, "psT", [P, 2, HALF])
        psO = psum(att, "psO", [P, 2, HALF])
        psA = psum(att, "psA", [P, 2, HALF])
        att.close()

        mlp = ExitStack()
        wp_h = sb(mlp, "wp_h", [P, KT, D], F32R)
        wp_l = sb(mlp, "wp_l", [P, KT, D], F32R)
        w1_h = sb(mlp, "w1_h", [P, KT, F], F32R)
        w1_l = sb(mlp, "w1_l", [P, KT, F], F32R)
        w2_h = sb(mlp, "w2_h", [P, FT, D], F32R)
        w2_l = sb(mlp, "w2_l", [P, FT, D], F32R)
        oin = sb(mlp, "oin", [P, 3, KT, RA])
        a_h = sb(mlp, "a_h", [P, 2, KT, RA], F32R)
        a_l = sb(mlp, "a_l", [P, 2, KT, RA], F32R)
        xc = sb(mlp, "xc", [P, NR, D])
        x1 = sb(mlp, "x1", [P, 2, NR, D])
        gate1 = sb(mlp, "gate1", [P, D])
        gate2 = sb(mlp, "gate2", [P, 2, D])
        bias1 = sb(mlp, "bias1", [P, 1, D])
        bias2 = sb(mlp, "bias2", [P, 1, D])
        tmp = sb(mlp, "tmp", [P, D])
        h_f = sb(mlp, "h_f", [P, 2, RA])
        h_h = sb(mlp, "h_h", [P, 4, RA], F32R)
        h_l = sb(mlp, "h_l", [P, 4, RA], F32R)
        stats2 = sb(mlp, "stats2", [P, NR, 6])
        aggr2 = sb(mlp, "aggr2", [P, NR, 2])
        rstd2 = sb(mlp, "rstd2", [P, NR])
        veps2 = sb(mlp, "veps2", [P, NR])
        psY = psum(mlp, "psY", [P, NR, D])
        psH = psum(mlp, "psH", [P, 4, D])
        psP = psum(mlp, "psP", [P, 2, D])
        yc = oin[:, 0]
        mlp.close()

        qk_loaded = [sem(f"qk_loaded{j}") for j in range(GH)]
        v_loaded = [sem(f"v_loaded{j}") for j in range(GH)]
        m_loaded = [sem(f"m_loaded{j}") for j in range(GH)]
        qk_stored = [sem(f"qk_stored{j}") for j in range(2)]
        v_stored = [sem(f"v_stored{j}") for j in range(2)]
        o_stored = [sem(f"o_stored{j}") for j in range(2)]
        NQKL = 6 * 16

        w1_v = W1.rearrange("(k p) f -> p k f", p=P)
        w2_v = W2.rearrange("(k p) d -> p k d", p=P)
        wp_v = Wproj.rearrange("(k p) d -> p k d", p=P)
        wq_v = Wqkv.rearrange("(k p) n -> p k n", p=P)
        wa_v = Wada.rearrange("(k p) n -> p k n", p=P)
        PIECES = [(wp_v[:, k:k + 2], wp_h[:, k:k + 2], wp_l[:, k:k + 2]) for k in range(0, KT, 2)]
        PIECES += [(w1_v[:, k, f:f + 1024], w1_h[:, k, f:f + 1024], w1_l[:, k, f:f + 1024])
                   for f in range(0, F, 1024) for k in range(KT)]
        PIECES += [(w2_v[:, k:k + 2], w2_h[:, k:k + 2], w2_l[:, k:k + 2]) for k in range(0, FT, 2)]

        def raw_piece(n, like):
            t = oin[:, n % 3].rearrange("p k r -> p (k r)")
            return t.rearrange("p (k r) -> p k r", k=2) if len(like.shape) == 3 else t

        def past(eng, name):
            eng.sem_inc(sem(f"past_{name}"), 1)

        block = keep.enter_context(nc.Block())

        @block.sync
        def _(sp):
            sp.dma_start(csb[:, 0], cond).then_inc(sem("cond_loaded"), 16)
            for n, v in enumerate((g1, be1, g2, be2)):
                sp.dma_start(gb[:, n], v).then_inc(sem("small_loaded"), 16)
            sp.dma_start(b1c[:], b1).then_inc(sem("small_loaded"), 16)

            def load_x(ia):
                wait(sp, sem("xn_ready"), ia)
                sp.dma_start(xin[:], x_rows[bass.ds(ia * RA, RA)].rearrange("(r p) d -> p r d", p=P))\
                  .then_inc(sem("x_loaded"), 16)

            sp.wait_ge(sem("ident_ready"), 2)
            load_x(0)
            for n in range(6):
                if n >= 2:
                    sp.wait_ge(sem("mod_turned"), n - 1)
                sp.dma_start(wada[:, n % 2], wa_v[:, :, n * D:(n + 1) * D]).then_inc(sem(f"wada_loaded{n % 2}"), 16)
                sp.dma_start(bada_sb[:, n % 2], bada[n * D:(n + 1) * D].partition_broadcast(B))\
                  .then_inc(sem(f"wada_loaded{n % 2}"), 16)
                sp.wait_ge(sem("mod_ready"), n + 1)
                if n < 2:
                    sp.dma_start(wraw[:, n], wq_v[:, n]).then_inc(sem(f"wraw_loaded{n}"), 16)
                sp.dma_start(mod_dram[n], mod[:, n % 2]).then_inc(sem(f"mod_stored{n % 2}"), 16)
            for k in range(2, KT):
                sp.wait_ge(sem("wqkv_lo"), k - 1)
                sp.dma_start(wraw[:, k % 2], wq_v[:, k]).then_inc(sem(f"wraw_loaded{k % 2}"), 16)

            for ia in range(1, AHEAD + 1):
                load_x(ia)

            def load_head(i, j):
                b, hg = (i // IPB, i % IPB) if isinstance(i, int) else (i // IPB, i % IPB)
                done = (b + 1) * IPB
                if j == 0:
                    for s in range(2):
                        wait(sp, qk_stored[s], done * (4 * 32))
                        past(sp, "sp")
                        wait(sp, v_stored[s], done * 16)
                        past(sp, "sp")
                rows = bass.ds(b * T, T)
                wait(sp, sem("scores_ready"), i * (GH * NSTEP) - (GH - 1 - j) * NSTEP
                     if not isinstance(i, int) or i > 0 else 0)
                for tile, kind, order in ((kst, 1, (0, 1, 0)), (qst, 0, (0, 0, 1))):
                    for s, hl in enumerate(order):
                        sp.dma_start(tile[HD * s:HD * (s + 1), j, :].bitcast(F32),
                                     qk_dram[kind, hg, hl, HD * j:HD * (j + 1), rows]
                                     if isinstance(i, int) else
                                     qk_dram[kind, bass.ds(hg, 1), hl, HD * j:HD * (j + 1), rows]
                                     .rearrange("a p r -> (a p) r"))\
                          .then_inc(qk_loaded[j], 16)
                wait(sp, sem("pv_done"), i * (GH * NSTEP) - (GH - 1 - j) * NSTEP
                     if not isinstance(i, int) or i > 0 else 0)
                src = v_dram[rows].rearrange("(k p) h c -> p k h c", p=P)
                if isinstance(i, int):
                    src = src[:, :, hg * GH + j]
                else:
                    src = src[:, :, bass.ds(hg * GH + j, 1)].rearrange("p k h c -> p k (h c)")
                sp.dma_start(vst[:, j].bitcast(F32), src).then_inc(v_loaded[j], 16)

            def place_max(i, j):
                wait(sp, sem("m_copied"), i * GH + j + 1)
                sp.dma_start(qst[96:97, j, :].bitcast(F32), m_row[:, j % 2, :].bitcast(F32)).then_inc(m_loaded[j], 16)

            for j in range(GH):
                load_head(0, j)
            place_max(0, 0)

            def turn(i, with_x):
                for j in range(GH):
                    place_max(i - 1 if j < 3 else i, (j + 1) % GH)
                    load_head(i, j)
                    if j == 2 and with_x:
                        load_x(i + AHEAD)

            with sp.Fori(1, NIT - AHEAD) as i:
                turn(i, True)
            with sp.Fori(NIT - AHEAD, NIT) as i:
                turn(i, False)
            for j in range(1, GH):
                place_max(NIT - 1, j)

            for s in range(2):
                sp.wait_ge(o_stored[s], 16 * NIT * GH)
            for n, (src, hi, _) in enumerate(PIECES):
                if n >= 3:
                    sp.wait_ge(sem("wmlp_lo"), n - 2)
                sp.dma_start(raw_piece(n, hi), src).then_inc(sem(f"wmlp_loaded{n % 3}"), 16)

            def load_rows(u, par, first=False):
                b = u // IPB
                rows = bass.ds(u * RA, RA)
                if first:
                    sp.wait_ge(sem("wmlp_lo"), len(PIECES))
                wait(sp, sem("y2_lo"), u)
                o_v = o_dram.rearrange("(k j) c r -> j c k r", j=GH)
                for j in range(GH):
                    for part in range(2):
                        sp.dma_start(oin[HD * j:HD * (j + 1), part],
                                     o_v[j, HD * part:HD * (part + 1), :, rows]).then_inc(sem("o_loaded"), 16)
                    sp.dma_start(oin[HD * j:HD * (j + 1), 2],
                                 o_v[j, 2 * HD, :, rows].partition_broadcast(HD)).then_inc(sem("o_loaded"), 16)
                wait(sp, sem("turned2"), 2 * u)
                sp.dma_start(xc[:], x_rows[rows].rearrange("(r p) d -> p r d", p=P)).then_inc(sem("xc_loaded"), 16)
                gate = [mod_dram[m, b] if isinstance(u, int) else mod_dram[m, bass.ds(b, 1)].rearrange("a d -> (a d)")
                        for m in (2, 5)]
                wait(sp, sem("x1_based"), u)
                for dst, src in ((gate1[:], gate[0]), (bias1[:, 0], bproj), (bias2[:, 0], b2)):
                    sp.dma_start(dst, src.partition_broadcast(P)).then_inc(sem("gate1_loaded"), 16)
                wait(sp, sem("y_added"), 2 * (u - 1) if not isinstance(u, int) or u > 0 else 0)
                sp.dma_start(gate2[:, par], gate[1].partition_broadcast(P)).then_inc(sem("gate2_loaded"), 16)

            for s in range(2):
                sp.wait_ge(sem(f"mod_stored{s}"), 48)
            load_rows(0, 0, True)
            load_rows(1, 1)

            def store_rows(u, par):
                sp.wait_ge(sem("y_added"), 2 * u + 2)
                sp.dma_start(out_rows[bass.ds(u * RA, RA)].rearrange("(r p) d -> p r d", p=P), x1[:, par])\
                  .then_inc(sem(f"out_stored{par}"), 16)

            with sp.Fori(0, NA // 2 - 1) as uu:
                for par in range(2):
                    store_rows(uu * 2 + par, par)
                    load_rows(uu * 2 + par + 2, par)
            for par in range(2):
                store_rows(NA - 2 + par, par)
            for par in range(2):
                sp.wait_ge(sem(f"out_stored{par}"), 16 * (NA // 2))

        @block.tensor
        def _(pe):
            pe.wait_ge(sem("ident_ready"), 2)
            pe.wait_ge(sem("silu_ready"), 1)
            for k in range(KT):
                mm = pe.transpose(psA[:, 0, k * B:(k + 1) * B], csb[:, 3, k * P:(k + 1) * P], ident[0:B, 0:B])
            mm.then_inc(sem("cond_turned"), 1)
            pe.wait_ge(sem("cond_copied"), 1)
            for n in range(6):
                pe.wait_ge(sem(f"wada_loaded{n % 2}"), 32 * (n // 2 + 1))
                for k in range(KT):
                    mm = pe.matmul(psA[0:B, (n + 1) % 2, :], sT[:, k, :], wada[:, n % 2, k, :],
                                   start=(k == 0), stop=(k == KT - 1))
                mm.then_inc(sem("mod_formed"), 1)
                pe.wait_ge(sem("mod_ready"), n + 1)
                for k in range(KT):
                    c = (n * KT + k) * B
                    mm = pe.transpose(psO[:, 0, c:c + B], mod[:, n % 2, k * P:(k + 1) * P], ident[0:B, 0:B])
                mm.then_inc(sem("mod_turned"), 1)

            def part_a_turn(ia):
                pe.wait_ge(sem("xn_ready"), ia + 1)
                for n in range(A_NTURN):
                    wait(pe, sem("a_lo_done"), ia * A_NITEM - 1 + n if not isinstance(ia, int) or ia > 0 else 0)
                    for k in range(2):
                        for r in range(NR):
                            mm = pe.transpose(psA[:, n, k * RA + r * P:k * RA + (r + 1) * P],
                                              xn[:, r, (2 * n + k) * P:(2 * n + k + 1) * P], ident[:])
                    mm.then_inc(sem("a_formed"), 1)

            def part_a(ia, name):
                idx = A_NTURN + A_ITEMS.index(name)
                if idx == A_NTURN:
                    pe.wait_ge(sem("xm_hi"), ia + 1)
                    pe.wait_ge(sem("xm_lo"), ia + 1)
                if idx < 2 * A_NTURN:
                    pe.wait_ge(sem("a_hi_done"), ia * A_N + idx - 1)
                else:
                    pe.wait_ge(sem("a_lo_done"), ia * A_NITEM + idx - A_NTURN - 1)
                n = 0
                for k in range(KT):
                    if name[0] == "v":
                        r = int(name[1:])
                        for a, w in ((xm_h, wqkv_h), (xm_h, wqkv_l), (xm_l, wqkv_h)):
                            mm = pe.matmul(psA[:, idx % 2, :], a[:, k, r * P:(r + 1) * P], w[:, k, 2 * D:3 * D],
                                           start=(n == 0), stop=(n == 3 * KT - 1))
                            n += 1
                    else:
                        m = int(name[2:])
                        for a, w in ((xm_h, wqkv_h), (xm_l, wqkv_h), (xm_h, wqkv_l)):
                            mm = pe.matmul(psA[:, idx % 2, 0:RA], w[:, k, m * P:(m + 1) * P], a[:, k, :],
                                           start=(n == 0), stop=(n == 3 * KT - 1))
                            n += 1
                mm.then_inc(sem("a_formed"), 1)

            def max_item(i, j, n):
                head = i * GH + j
                if n == 0:
                    pe.wait_ge(qk_loaded[j], (i + 1) * NQKL)
                wait(pe, sem("max_done"), head * NMAX + n - 1)
                bank = psS[:, (j + n) % 2, :]
                if n == NMAX - 1:
                    pe.wait_ge(sem("max_joined"), head + 1)
                    pe.transpose(bank[0:8, 0:P], mxc[:], ident[:]).then_inc(sem("max_formed"), 1)
                    return
                qt, part, k0, w = MAXES[n]
                diag = k0 + w == P * (qt + 1)
                mm = pe.matmul(bank[:, 0:w], qst[0:96, j, qt * P:(qt + 1) * P], kst[0:96, j, k0:k0 + w],
                               start=True, stop=True)
                if diag:
                    mm = pe.matmul(bank[:, w - P:w], ident_b[:], mask_q[:], start=False, stop=True,
                                   skip_group_check=True)
                mm.then_inc(sem("max_formed"), 1)

            def scores(i, j, c):
                n = i * (GH * NSTEP) + j * NSTEP + c
                if c == 0:
                    pe.wait_ge(m_loaded[j], (i + 1) * 16)
                wait(pe, sem("exp_done"), n - 1)
                _, kt, q0, w = CHUNKS[c]
                bank = psT[:, c % 2, :]
                diag = q0 == P * kt
                mm = pe.matmul(bank[:, 0:w], kst[0:97, j, kt * P:(kt + 1) * P], qst[0:97, j, q0:q0 + w],
                               start=True, stop=True)
                if diag:
                    mm = pe.matmul(bank[:, 0:P], ident_b[:], mask_k[:], start=False, stop=True,
                                   skip_group_check=True)
                mm.then_inc(sem("scores_ready"), 1)

            def values(i, j, c):
                n = i * (GH * NSTEP) + j * NSTEP + c
                half, kt, q0, w = CHUNKS[c]
                if c == 0:
                    pe.wait_ge(v_loaded[j], (i + 1) * 16)
                if kt == 0:
                    wait(pe, sem("o_copied"), (i * GH + j) * 2 + half - 1)
                pe.wait_ge(sem("prob_hi"), n + 1)
                pe.wait_ge(sem("prob_lo"), n + 1)
                o = psO[0:VW, half, q0 - HALF * half:q0 - HALF * half + w]
                pe.matmul(o, vst[:, j, kt, :], e_h[:, c % RING, 0:w], start=(kt == 0), stop=True,
                          skip_group_check=True)
                pe.matmul(o, vst[:, j, kt, :], e_l[:, c % RING, 0:w], start=False, stop=True,
                          skip_group_check=True).then_inc(sem("pv_done"), 1)

            def iteration(i, with_a, last):
                for s in range(GH * NSTEP):
                    j, c = divmod(s, NSTEP)
                    scores(i, j, c)
                    if not (last and j == GH - 1):
                        for n in MAX_AT.get(c, ()):
                            max_item(i + (j + 1) // GH, (j + 1) % GH, n)
                    if with_a and s == LN_TURN_AT:
                        part_a_turn(i + AHEAD)
                    if with_a and s in A_AT:
                        part_a(i + AHEAD, A_AT[s])
                    if s >= LAG:
                        values(i, *divmod(s - LAG, NSTEP))
                for s in range(GH * NSTEP - LAG, GH * NSTEP):
                    values(i, *divmod(s, NSTEP))

            def a_alone(ia):
                part_a_turn(ia)
                for name in A_ITEMS:
                    part_a(ia, name)

            pe.wait_ge(sem("wqkv_hi"), KT)
            pe.wait_ge(sem("wqkv_lo"), KT)
            a_alone(0)
            with pe.Fori(1, AHEAD) as ia:
                a_alone(ia)
            pe.wait_ge(sem("kst_set"), 1)
            pe.wait_ge(sem("masks_ready"), 2)
            for n in range(NMAX):
                max_item(0, 0, n)
            iteration(0, True, False)
            with pe.Fori(1, NIT - AHEAD) as i:
                iteration(i, True, False)
            with pe.Fori(NIT - AHEAD, NIT - 1) as i:
                iteration(i, False, False)
            iteration(NIT - 1, False, True)

            def project(u, par):
                pe.wait_ge(sem("att_hi"), u + 1)
                pe.wait_ge(sem("att_lo"), u + 1)
                for r in range(NR):
                    wait(pe, sem("y2_done"), 2 * (u - 1) + r + 1 if not isinstance(u, int) or u > 0 else 0)
                    n = 0
                    for k in range(KT):
                        for a, w in ((a_h, wp_h), (a_h, wp_l), (a_l, wp_h)):
                            mm = pe.matmul(psP[:, r, :], a[:, par, k, r * P:(r + 1) * P], w[:, k, :],
                                           start=(n == 0), stop=(n == 3 * KT - 1))
                            n += 1
                    mm.then_inc(sem("projected"), 1)

            def turn2(u, par):
                pe.wait_ge(sem("xn2_ready"), u + 1)
                for n in range(2):
                    for k in range(2):
                        for r in range(NR):
                            mm = pe.transpose(psP[:, n, k * RA + r * P:k * RA + (r + 1) * P],
                                              xc[:, r, (2 * n + k) * P:(2 * n + k + 1) * P], ident[:])
                    mm.then_inc(sem("turned2"), 1)

            def hidden(u, par, m):
                if m == 0:
                    pe.wait_ge(sem("rows_hi"), u + 1)
                    pe.wait_ge(sem("rows_lo"), u + 1)
                wait(pe, sem("gelu_done"), u * FT + m - 3)
                n = 0
                for k in range(KT):
                    for w, a in ((w1_h, a_h), (w1_h, a_l), (w1_l, a_h)):
                        mm = pe.matmul(psH[:, m % 4, 0:RA], w[:, k, m * P:(m + 1) * P], a[:, par, k, :],
                                       start=(n == 0), stop=(n == 3 * KT - 1))
                        n += 1
                mm.then_inc(sem("hidden_ready"), 1)

            def mlp_out(u, m):
                if m == 0:
                    wait(pe, sem("y_added"), 2 * u)
                pe.wait_ge(sem("h_hi"), u * FT + m + 1)
                pe.wait_ge(sem("h_lo"), u * FT + m + 1)
                for r in range(NR):
                    for n, (a, w) in enumerate(((h_h, w2_h), (h_h, w2_l), (h_l, w2_h))):
                        mm = pe.matmul(psY[:, r, :], a[:, m % 4, r * P:(r + 1) * P], w[:, m, :],
                                       start=(m == 0 and n == 0), stop=(m == FT - 1 and n == 2),
                                       skip_group_check=True)
                mm.then_inc(sem("mlp_done"), 1)

            def rows(u, par, prepare):
                for m in range(FT):
                    hidden(u, par, m)
                    if prepare and m == 3:
                        project(u + 1, 1 - par)
                    if prepare and m == 9:
                        turn2(u + 1, 1 - par)
                    if m >= 2:
                        mlp_out(u, m - 2)
                for m in range(FT - 2, FT):
                    mlp_out(u, m)

            pe.wait_ge(sem("wmlp_hi"), len(PIECES))
            pe.wait_ge(sem("wmlp_lo"), len(PIECES))
            project(0, 0)
            turn2(0, 0)
            for par in range(2):
                rows(par, par, True)
            with pe.Fori(1, NA // 2 - 1) as uu:
                for par in range(2):
                    rows(uu * 2 + par, par, True)
            rows(NA - 2, 0, True)
            rows(NA - 1, 1, False)

        @block.scalar
        def _(act):
            act.wait_ge(sem("cond_loaded"), 16)
            act.activation(csb[:, 1], csb[:, 0], ACT.Exp, scale=-1.0).then_inc(sem("cond_exp"), 1)
            act.wait_ge(sem("cond_turned"), 1)
            act.activation(sT[:].rearrange("p k b -> p (k b)"), psA[:, 0, 0:KT * B], ACT.Copy)\
               .then_inc(sem("cond_copied"), 1)

            def a_modulate(ia):
                b = ia // IPB
                wait(act, sem("xm_hi"), ia)
                wait(act, sem("xm_lo"), ia)
                for n in range(A_NTURN):
                    act.wait_ge(sem("a_formed"), ia * A_N + n + 1)
                    for k in range(2):
                        kk = 2 * n + k
                        ca, cb = (coef[:, w, b, kk:kk + 1] if isinstance(ia, int) else
                                  coef[:, w, bass.ds(b, 1), kk] for w in (0, 1))
                        a = act.activation(yT[:, kk, :], psA[:, n, k * RA:(k + 1) * RA], ACT.Identity,
                                           scale=ca, bias=cb)
                    a.then_inc(sem("a_hi_done"), 1)

            def a_high(ia, name):
                idx = A_NTURN + A_ITEMS.index(name)
                if name[0] == "v":
                    r = int(name[1:])
                    wait(act, v_stored[r], ia * 16)
                    dst = vaug[:, r, :, 0:HD]
                    src = psA[:, idx % 2, :].rearrange("p (h c) -> p h c", c=HD)
                else:
                    m = int(name[2:])
                    wait(act, qk_stored[m % 2], ia * (4 * 32) + (m // 2) * 32)
                    dst, src = qk_h[:, m % 2, :], psA[:, idx % 2, 0:RA]
                act.wait_ge(sem("a_formed"), ia * A_N + idx + 1)
                act.activation(dst, src, ACT.Copy).then_inc(sem("a_hi_done"), 1)

            def a_store(ia, name):
                idx = A_ITEMS.index(name)
                act.wait_ge(sem("a_hi_done"), ia * A_N + A_NTURN + idx + 1)
                act.wait_ge(sem("a_lo_done"), ia * A_NITEM + idx + 1)
                if name[0] == "v":
                    r = int(name[1:])
                    act.dma_start(v_dram[bass.ds(ia * RA + r * P, P)].rearrange("p h c -> p (h c)"),
                                  vaug[:, r].rearrange("p h c -> p (h c)").bitcast(F32)).then_inc(v_stored[r], 16)
                else:
                    m = int(name[2:])
                    for hl, t in enumerate((qk_h, qk_l)):
                        act.dma_start(qk_dram[m // IPB, m % IPB, hl, :, bass.ds(ia * RA, RA)], t[:, m % 2, :].bitcast(F32))\
                           .then_inc(qk_stored[m % 2], 16)

            def part_a(ia, name):
                a_high(ia, name)
                at = A_ITEMS.index(name)
                if at:
                    a_store(ia, A_ITEMS[at - 1])

            def exps(i, j, c):
                n = i * (GH * NSTEP) + j * NSTEP + c
                w = CHUNKS[c][3]
                wait(act, sem("prob_lo"), n - RING + 1)
                act.wait_ge(sem("scores_ready"), n + 1)
                act.activation(e_f[:, c % RING, 0:w], psT[:, c % 2, 0:w], ACT.Exp, scale=SCALE)\
                   .then_inc(sem("exp_done"), 1)

            def o_copy(i, j, half):
                head = i * GH + j
                wait(act, o_stored[half], head * 16)
                act.wait_ge(sem("pv_done"), head * NSTEP + (4 if half == 0 else NSTEP))
                act.activation(o_sb[:, half, :], psO[0:VW, half, :], ACT.Copy).then_inc(sem("o_copied"), 1)

            def o_store(i, j, half):
                act.wait_ge(sem("o_copied"), (i * GH + j) * 2 + half + 1)
                b, hg = i // IPB, i % IPB
                cols = bass.ds(b * T + half * HALF, HALF)
                dst = o_dram[hg * GH + j, :, cols] if isinstance(i, int) else \
                    o_dram[bass.ds(hg * GH + j, 1), :, cols].rearrange("a c r -> (a c) r")
                act.dma_start(dst, o_sb[:, half, :]).then_inc(o_stored[half], 16)

            def iteration(i, with_a, last):
                for s in range(GH * NSTEP + LAG + 2):
                    for half, end in ((0, 4), (1, NSTEP)):
                        j, c = divmod(s - end - LAG, NSTEP)
                        if c == 0 and 0 <= j < GH:
                            o_copy(i, j, half)
                        j, c = divmod(s - end - LAG - 1, NSTEP)
                        if c == 0 and 0 <= j < GH:
                            o_store(i, j, half)
                    if s < GH * NSTEP:
                        exps(i, *divmod(s, NSTEP))
                        if with_a and s == LN_TURN_AT:
                            a_modulate(i + AHEAD)
                        if with_a and s in A_AT:
                            part_a(i + AHEAD, A_AT[s])
                if with_a:
                    a_store(i + AHEAD, A_ITEMS[-1])

            def a_alone(ia):
                a_modulate(ia)
                for name in A_ITEMS:
                    part_a(ia, name)
                a_store(ia, A_ITEMS[-1])

            act.wait_ge(sem("coef_ready"), 1)
            a_alone(0)
            with act.Fori(1, AHEAD) as ia:
                a_alone(ia)
            iteration(0, True, False)
            with act.Fori(1, NIT - AHEAD) as i:
                iteration(i, True, False)
            with act.Fori(NIT - AHEAD, NIT) as i:
                iteration(i, False, False)

            def modulate2(u):
                b = u // IPB
                for n in range(2):
                    act.wait_ge(sem("turned2"), 2 * u + n + 1)
                    if n == 0:
                        act.wait_ge(sem("att_lo"), u + 1)
                    for k in range(2):
                        kk = 2 * n + k
                        ca, cb = (coef[:, w, b, kk:kk + 1] if isinstance(u, int) else
                                  coef[:, w, bass.ds(b, 1), kk] for w in (2, 3))
                        a = act.activation(yc[:, kk, :], psP[:, n, k * RA:(k + 1) * RA], ACT.Identity,
                                           scale=ca, bias=cb)
                    a.then_inc(sem("y2_done"), 1)

            def gelu(u, m):
                wait(act, sem("h_lo"), u * FT + m - 1)
                act.wait_ge(sem("hidden_ready"), u * FT + m + 1)
                act.activation(h_f[:, m % 2, :], psH[:, m % 4, 0:RA], ACT.Gelu, bias=b1c[:, m:m + 1])\
                   .then_inc(sem("gelu_done"), 1)

            def rows(u, prepare):
                for m in range(FT):
                    gelu(u, m)
                    if prepare and m == 9:
                        modulate2(u + 1)

            act.wait_ge(sem("small_loaded"), 5 * 16)
            modulate2(0)
            rows(0, True)
            with act.Fori(1, NA - 1) as u:
                rows(u, True)
            rows(NA - 1, False)

        @block.vector
        def _(dve):
            dve.memset(mx[:], LOWEST).then_inc(sem("mx_set"), 1)
            dve.memset(kst[96:97].bitcast(F32), -1.0).then_inc(sem("kst_set"), 1)
            dve.wait_ge(sem("cond_exp"), 1)
            dve.tensor_scalar_add(csb[:, 1], csb[:, 1], 1.0).then_inc(sem("silu_step"), 1)
            dve.wait_ge(sem("silu_step"), 1)
            dve.reciprocal(csb[:, 2], csb[:, 1]).then_inc(sem("silu_step"), 1)
            dve.wait_ge(sem("silu_step"), 2)
            dve.tensor_tensor(csb[:, 3], csb[:, 0], csb[:, 2], ALU.mult).then_inc(sem("silu_ready"), 1)

            def wqkv_high(k):
                dve.wait_ge(sem(f"wraw_loaded{k % 2}"), 16 * (k // 2 + 1))
                dve.tensor_copy(wqkv_h[:, k, :], wraw[:, k % 2, :]).then_inc(sem("wqkv_hi"), 1)

            for n in range(6):
                dve.wait_ge(sem("mod_formed"), n + 1)
                if n >= 2:
                    dve.wait_ge(sem(f"mod_stored{n % 2}"), 16 * (n // 2))
                    dve.wait_ge(sem("mod_turned"), n - 1)
                dve.wait_ge(sem(f"wada_loaded{n % 2}"), 32 * (n // 2 + 1))
                dve.tensor_tensor(mod[:, n % 2], psA[0:B, (n + 1) % 2, :], bada_sb[:, n % 2], ALU.add)\
                   .then_inc(sem("mod_ready"), 1)
            for k in range(KT):
                wqkv_high(k)

            dve.wait_ge(sem("mod_turned"), 6)
            dve.wait_ge(sem("small_loaded"), 5 * 16)
            turned = psO[:, 0, 0:6 * KT * B].rearrange("p (n k b) -> p n k b", n=6, k=KT)
            for c, (shift, scale) in enumerate(((0, 1), (3, 4))):
                for k in range(KT):
                    dve.tensor_scalar(coef[:, 2 * c, :, k], turned[:, scale, k, :], 1.0, gb[:, 2 * c, k:k + 1],
                                      ALU.add, ALU.mult).then_inc(sem("coef_step"), 1)
                    a = dve.tensor_scalar(coef[:, 2 * c + 1, :, k], turned[:, scale, k, :], 1.0,
                                          gb[:, 2 * c + 1, k:k + 1], ALU.add, ALU.mult)
                    a.then_inc(sem("coef_step"), 1)
            dve.wait_ge(sem("coef_step"), 4 * KT)
            for c, (shift, scale) in enumerate(((0, 1), (3, 4))):
                a = dve.tensor_tensor(coef[:, 2 * c + 1].rearrange("p b k -> p k b"),
                                      coef[:, 2 * c + 1].rearrange("p b k -> p k b"), turned[:, shift], ALU.add)
                a.then_inc(sem("coef_step"), 1)
            dve.wait_ge(sem("coef_step"), 4 * KT + 2)
            dve.sem_inc(sem("coef_ready"), 1)

            def normalise(ia):
                dve.wait_ge(sem("x_loaded"), 16 * (ia + 1))
                for r in range(NR):
                    dve.bn_stats(stats[:, r], xin[:, r]).then_inc(sem("ln_stats"), 1)
                for r in range(NR):
                    dve.wait_ge(sem("ln_stats"), ia * NR + r + 1)
                    past(dve, "dve")
                    dve.bn_aggr(aggr[:, r], stats[:, r]).then_inc(sem("ln_aggr"), 1)
                dve.wait_ge(sem("ln_aggr"), ia * NR + NR)
                dve.tensor_scalar_add(veps[:], aggr[:, :, 1], EPS).then_inc(sem("ln_veps"), 1)
                dve.wait_ge(sem("ln_rstd"), ia + 1)
                wait(dve, sem("a_formed"), ia * A_N - A_NITEM if not isinstance(ia, int) or ia > 0 else 0)
                for r in range(NR):
                    a = dve.tensor_scalar(xn[:, r], xin[:, r], aggr[:, r, 0:1], rstd[:, r:r + 1],
                                          ALU.subtract, ALU.mult)
                a.then_inc(sem("xn_ready"), 1)

            def a_split(ia):
                dve.wait_ge(sem("a_hi_done"), ia * A_N + A_NTURN)
                wait(dve, sem("a_formed"), ia * A_N)
                dve.tensor_copy(xm_h[:], yT[:]).then_inc(sem("xm_hi"), 1)

            def a_low(ia, name):
                idx = A_NTURN + A_ITEMS.index(name)
                dve.wait_ge(sem("a_hi_done"), ia * A_N + idx + 1)
                if name[0] == "v":
                    r = int(name[1:])
                    src = psA[:, idx % 2, :].rearrange("p (h c) -> p h c", c=HD)
                    hi, lo = vaug[:, r, :, 0:HD], vaug[:, r, :, HD:2 * HD]
                else:
                    m = int(name[2:])
                    src, hi, lo = psA[:, idx % 2, 0:RA], qk_h[:, m % 2, :], qk_l[:, m % 2, :]
                dve.tensor_tensor(lo, src, hi.bitcast(F32), ALU.subtract).then_inc(sem("a_lo_done"), 1)

            def max_item(i, j, n):
                head = i * GH + j
                if n == NMAX - 1:
                    dve.wait_ge(sem("max_done"), head * NMAX + n)
                    dve.tensor_tensor(mxc[:], mx[:, 0], mx[:, 1], ALU.max).then_inc(sem("max_joined"), 1)
                    slot = (j - 2) % GH
                    wait(dve, m_loaded[slot], (i + (j - 2) // GH + 1) * 16)
                    dve.wait_ge(sem("max_formed"), head * NMAX + n + 1)
                    a = dve.tensor_copy(m_row[:, j % 2, :], psS[0:8, (j + n) % 2, 0:P])
                    a.then_inc(sem("m_copied"), 1)
                    dve.wait_ge(sem("m_copied"), head + 1)
                    dve.sem_inc(sem("max_done"), 1)
                    return
                qt, part, _, w = MAXES[n]
                if n == 0:
                    wait(dve, sem("max_joined"), head)
                dve.wait_ge(sem("max_formed"), head * NMAX + n + 1)
                dve.tensor_reduce(mx[:, part, qt:qt + 1], psS[:, (j + n) % 2, 0:w], AX_X, ALU.max)\
                   .then_inc(sem("max_done"), 1)

            def prob_low(i, j, c):
                n = i * (GH * NSTEP) + j * NSTEP + c
                w = CHUNKS[c][3]
                dve.wait_ge(sem("prob_hi"), n + 1)
                dve.tensor_tensor(e_l[:, c % RING, 0:w], e_f[:, c % RING, 0:w], e_h[:, c % RING, 0:w].bitcast(F32),
                                  ALU.subtract).then_inc(sem("prob_lo"), 1)

            def iteration(i, with_a, last):
                for s in range(GH * NSTEP + LOW_LAG):
                    j, c = divmod(s, NSTEP)
                    if s < GH * NSTEP and not (last and j == GH - 1):
                        for n in MAX_AT.get(c, ()):
                            max_item(i + (j + 1) // GH, (j + 1) % GH, n)
                    if with_a and s == LN_STATS_AT:
                        normalise(i + AHEAD)
                    if with_a and s == LN_SPLIT_AT:
                        a_split(i + AHEAD)
                    if s >= LOW_LAG:
                        prob_low(i, *divmod(s - LOW_LAG, NSTEP))
                    if with_a and s in A_AT:
                        a_low(i + AHEAD, A_AT[s])

            def a_alone(ia):
                normalise(ia)
                a_split(ia)
                for name in A_ITEMS:
                    a_low(ia, name)

            dve.wait_ge(sem("ones_set"), 2)
            a_alone(0)
            with dve.Fori(1, AHEAD) as ia:
                a_alone(ia)
            dve.wait_ge(sem("mx_set"), 1)
            for n in range(NMAX):
                max_item(0, 0, n)
            iteration(0, True, False)
            with dve.Fori(1, NIT - AHEAD) as i:
                iteration(i, True, False)
            with dve.Fori(NIT - AHEAD, NIT - 1) as i:
                iteration(i, False, False)
            iteration(NIT - 1, False, True)

            for n, (_, hi, _) in enumerate(PIECES):
                dve.wait_ge(sem(f"wmlp_loaded{n % 3}"), 16 * (n // 3 + 1))
                dve.tensor_copy(hi, raw_piece(n, hi)).then_inc(sem("wmlp_hi"), 1)

            def attended(u, par):
                dve.wait_ge(sem("o_loaded"), 12 * 16 * (u + 1))
                dve.tensor_tensor(oin[:, 0], oin[:, 0], oin[:, 1], ALU.add).then_inc(sem("att_step"), 1)
                dve.reciprocal(oin[:, 2], oin[:, 2]).then_inc(sem("att_step"), 1)
                dve.wait_ge(sem("att_step"), 2 * u + 2)
                dve.tensor_tensor(oin[:, 0], oin[:, 0], oin[:, 2], ALU.mult).then_inc(sem("att_ready"), 1)
                dve.wait_ge(sem("att_ready"), u + 1)
                wait(dve, sem("hidden_ready"), (u - 1) * FT if not isinstance(u, int) or u > 1 else 0)
                dve.tensor_copy(a_h[:, par], oin[:, 0]).then_inc(sem("att_hi"), 1)

            def residual(u, par):
                dve.wait_ge(sem("xc_loaded"), 16 * (u + 1))
                dve.wait_ge(sem("gate1_loaded"), 48 * (u + 1))
                dve.wait_ge(sem("gate2_loaded"), 16 * (u + 1))
                dve.tensor_tensor(bias1[:, 0], bias1[:, 0], gate1[:], ALU.mult).then_inc(sem("bias_step"), 1)
                dve.tensor_tensor(bias2[:, 0], bias2[:, 0], gate2[:, par], ALU.mult).then_inc(sem("bias_step"), 1)
                dve.wait_ge(sem("bias_step"), 2 * u + 2)
                dve.tensor_tensor(xc[:], xc[:], bias1[:].to_broadcast([P, NR, D]), ALU.add)\
                   .then_inc(sem("xc_based"), 1)
                for r in range(NR):
                    dve.wait_ge(sem("projected"), u * NR + r + 1)
                    wait(dve, sem("x1_step"), u * NR + r)
                    dve.tensor_tensor(tmp[:], psP[:, r], gate1[:], ALU.mult).then_inc(sem("gated"), 1)
                    dve.wait_ge(sem("gated"), u * NR + r + 1)
                    if r == 0:
                        dve.wait_ge(sem("xc_based"), u + 1)
                        v = (u // 2) * 16 if isinstance(u, int) else u * 8 - 8 * par
                        wait(dve, sem(f"out_stored{par}"), v)
                    dve.tensor_tensor(x1[:, par, r], xc[:, r], tmp[:], ALU.add).then_inc(sem("x1_step"), 1)
                for r in range(NR):
                    dve.wait_ge(sem("x1_step"), u * NR + r + 1)
                    dve.bn_stats(stats2[:, r], x1[:, par, r]).then_inc(sem("ln2_stats"), 1)
                for r in range(NR):
                    dve.wait_ge(sem("ln2_stats"), u * NR + r + 1)
                    past(dve, "dve")
                    dve.bn_aggr(aggr2[:, r], stats2[:, r]).then_inc(sem("ln2_aggr"), 1)
                dve.wait_ge(sem("ln2_aggr"), u * NR + NR)
                dve.tensor_scalar_add(veps2[:], aggr2[:, :, 1], EPS).then_inc(sem("ln2_veps"), 1)
                dve.wait_ge(sem("ln2_rstd"), u + 1)
                for r in range(NR):
                    a = dve.tensor_scalar(xc[:, r], x1[:, par, r], aggr2[:, r, 0:1], rstd2[:, r:r + 1],
                                          ALU.subtract, ALU.mult)
                a.then_inc(sem("xn2_ready"), 1)
                dve.wait_ge(sem("xn2_ready"), u + 1)
                dve.tensor_tensor(x1[:, par], x1[:, par], bias2[:].to_broadcast([P, NR, D]), ALU.add)\
                   .then_inc(sem("x1_based"), 1)

            def rows_high(u, par):
                dve.wait_ge(sem("y2_done"), 2 * u + 2)
                dve.wait_ge(sem("projected"), 2 * u + 2)
                dve.tensor_copy(a_h[:, par], yc[:]).then_inc(sem("rows_hi"), 1)

            def hidden_high(u, m):
                n = u * FT + m
                wait(dve, sem("mlp_done"), n - 3)
                dve.wait_ge(sem("gelu_done"), n + 1)
                dve.tensor_copy(h_h[:, m % 4, :], h_f[:, m % 2, :]).then_inc(sem("h_hi"), 1)

            def finish(u, par):
                for r in range(NR):
                    dve.wait_ge(sem("mlp_done"), (u + 1) * FT)
                    dve.tensor_tensor(tmp[:], psY[:, r], gate2[:, par], ALU.mult).then_inc(sem("gated2"), 1)
                    dve.wait_ge(sem("gated2"), u * NR + r + 1)
                    dve.tensor_tensor(x1[:, par, r], x1[:, par, r], tmp[:], ALU.add).then_inc(sem("y_added"), 1)
                    dve.wait_ge(sem("y_added"), u * NR + r + 1)

            def rows(u, par, prepare):
                for m in range(FT):
                    if prepare and m == 2:
                        attended(u + 1, 1 - par)
                    if prepare and m == 4:
                        residual_first(u + 1, 1 - par)
                    if prepare and m == 10:
                        rows_high(u + 1, 1 - par)
                    hidden_high(u, m)
                finish(u, par)

            residual_first = residual
            attended(0, 0)
            residual(0, 0)
            rows_high(0, 0)
            for par in range(2):
                rows(par, par, True)
            with dve.Fori(1, NA // 2 - 1) as uu:
                for par in range(2):
                    rows(uu * 2 + par, par, True)
            rows(NA - 2, 0, True)
            rows(NA - 1, 1, False)

        @block.gpsimd
        def _(pool):
            pool.memset(ident[:], 0.0).then_inc(sem("pool_set"), 1)
            pool.memset(ident_b[:], 0.0).then_inc(sem("pool_set"), 1)
            pool.memset(mask_q[:], 0.0).then_inc(sem("pool_set"), 1)
            pool.memset(mask_k[:], 0.0).then_inc(sem("pool_set"), 1)
            pool.memset(power[:], -0.5).then_inc(sem("pool_set"), 1)
            pool.wait_ge(sem("pool_set"), 5)
            pool.affine_select(out=ident[:], in_=ident[:], compare_op=ALU.not_equal, fill=1.0, base=0,
                               pattern=[[-1, P]], channel_multiplier=1).then_inc(sem("ident_ready"), 1)
            pool.affine_select(out=ident_b[:], in_=ident_b[:], compare_op=ALU.not_equal, fill=1.0, base=0,
                               pattern=[[-1, P]], channel_multiplier=1).then_inc(sem("ident_ready"), 1)
            for r in range(NR):
                pool.memset(vaug[:, r, :, 2 * HD:VW].bitcast(F32), 1.0).then_inc(sem("ones_set"), 1)
            pool.affine_select(out=mask_q[:], in_=mask_q[:], compare_op=ALU.is_ge, fill=MASKED, base=0,
                               pattern=[[-1, P]], channel_multiplier=1).then_inc(sem("masks_ready"), 1)
            pool.affine_select(out=mask_k[:], in_=mask_k[:], compare_op=ALU.is_ge, fill=MASKED, base=0,
                               pattern=[[1, P]], channel_multiplier=-1).then_inc(sem("masks_ready"), 1)

            def low(dst, full, high):
                return pool.tensor_tensor(dst, full, high.bitcast(F32), ALU.subtract)

            pool.wait_ge(sem("masks_ready"), 2)
            for k in range(KT):
                pool.wait_ge(sem("wqkv_hi"), k + 1)
                low(wqkv_l[:, k, :], wraw[:, k % 2, :], wqkv_h[:, k, :]).then_inc(sem("wqkv_lo"), 1)

            def a_rstd(ia):
                pool.wait_ge(sem("ln_veps"), ia + 1)
                pool.tensor_tensor(rstd[:], veps[:], power[:], ALU.pow).then_inc(sem("ln_rstd"), 1)

            def a_split(ia):
                pool.wait_ge(sem("xm_hi"), ia + 1)
                low(xm_l[:], yT[:], xm_h[:]).then_inc(sem("xm_lo"), 1)

            def prob_high(i, j, c):
                n = i * (GH * NSTEP) + j * NSTEP + c
                w = CHUNKS[c][3]
                wait(pool, sem("pv_done"), n - RING + 1)
                pool.wait_ge(sem("exp_done"), n + 1)
                past(pool, "pool")
                pool.tensor_scalar(e_h[:, c % RING, 0:w], e_f[:, c % RING, 0:w], 1.0, 1.0, ALU.mult, ALU.mult)\
                    .then_inc(sem("prob_hi"), 1)

            def iteration(i, with_a):
                for s in range(GH * NSTEP):
                    prob_high(i, *divmod(s, NSTEP))
                    if with_a and s == LN_STATS_AT:
                        a_rstd(i + AHEAD)
                    if with_a and s == LN_SPLIT_AT:
                        a_split(i + AHEAD)

            a_rstd(0)
            a_split(0)
            with pool.Fori(1, AHEAD) as ia:
                a_rstd(ia)
                a_split(ia)
            iteration(0, True)
            with pool.Fori(1, NIT - AHEAD) as i:
                iteration(i, True)
            with pool.Fori(NIT - AHEAD, NIT) as i:
                iteration(i, False)

            for n, (_, hi, lo) in enumerate(PIECES):
                pool.wait_ge(sem("wmlp_hi"), n + 1)
                low(lo, raw_piece(n, hi), hi).then_inc(sem("wmlp_lo"), 1)

            def attended(u, par):
                pool.wait_ge(sem("att_hi"), u + 1)
                low(a_l[:, par], oin[:, 0], a_h[:, par]).then_inc(sem("att_lo"), 1)

            def rstd_2(u):
                pool.wait_ge(sem("ln2_veps"), u + 1)
                pool.tensor_tensor(rstd2[:], veps2[:], power[:], ALU.pow).then_inc(sem("ln2_rstd"), 1)

            def rows_low(u, par):
                pool.wait_ge(sem("rows_hi"), u + 1)
                low(a_l[:, par], yc[:], a_h[:, par]).then_inc(sem("rows_lo"), 1)
                pool.wait_ge(sem("rows_lo"), u + 1)
                pool.sem_inc(sem("y2_lo"), 1)

            def hidden_low(u, m):
                pool.wait_ge(sem("h_hi"), u * FT + m + 1)
                low(h_l[:, m % 4, :], h_f[:, m % 2, :], h_h[:, m % 4, :]).then_inc(sem("h_lo"), 1)

            def rows(u, par, prepare):
                for m in range(FT):
                    if prepare and m == 2:
                        attended(u + 1, 1 - par)
                    if prepare and m == 4:
                        rstd_2(u + 1)
                    if prepare and m == 10:
                        rows_low(u + 1, 1 - par)
                    hidden_low(u, m)

            attended(0, 0)
            rstd_2(0)
            rows_low(0, 0)
            with pool.Fori(0, NA // 2 - 1) as uu:
                for par in range(2):
                    rows(uu * 2 + par, par, True)
            rows(NA - 2, 0, True)
            rows(NA - 1, 1, False)


_INS = ['x', 'cond_1024', 'L0_cond_Wqkv', 'L0_cond_Wproj', 'L0_cond_bproj', 'L0_cond_W1', 'L0_cond_b1',
        'L0_cond_W2', 'L0_cond_b2', 'L0_cond_g1', 'L0_cond_be1', 'L0_cond_g2', 'L0_cond_be2', 'L0_cond_Wada',
        'L0_cond_bada']
_BY_PARTITION = ['L0_cond_b1', 'L0_cond_g1', 'L0_cond_be1', 'L0_cond_g2', 'L0_cond_be2']
_OUTS = [((8, 1024, 512), 'float32')]


def kernel(**inputs):
    import numpy as _np
    import concourse.bacc as _bacc
    from concourse import mybir as _mybir
    from concourse.bass_utils import run_bass_kernel_spmd as _run

    nc = _bacc.Bacc("TRN2", target_bir_lowering=False, num_devices=1)
    arrays, args = {}, []
    for name in _INS:
        a = _np.ascontiguousarray(inputs[name])
        if name in _BY_PARTITION:
            a = _np.ascontiguousarray(a.reshape(-1, P).T)
        arrays[f"in_{name}_dram"] = a
        args.append(nc.dram_tensor(f"in_{name}_dram", a.shape, _mybir.dt.from_np(a.dtype), kind="ExternalInput").ap())
    for i, (shape, dtype) in enumerate(_OUTS):
        dt = _mybir.dt.from_np(_np.dtype(dtype))
        args.append(nc.dram_tensor(f"out_{i}_dram", shape, dt, kind="ExternalOutput").ap())
    build(nc, *args)
    r = _run(nc, [arrays], core_ids=[0])
    got = tuple(r.results[0][f"out_{i}_dram"] for i in range(len(_OUTS)))
    return got[0]
```

```python
from contextlib import ExitStack

import concourse.bass as bass
from concourse import mybir

ALU = mybir.AluOpType
ACT = mybir.ActivationFunctionType
AX_X = mybir.AxisListType.X
F32 = mybir.dt.float32
F32R = mybir.dt.float32r
BF16 = mybir.dt.bfloat16

P = 128
EPS = 1e-5
MASKED = -1e30
LOWEST = -3e38

GH = 4
RA = 256
AHEAD = 5
HALF = 512
NSTEP = 12
STEPS = GH * NSTEP
RING = 8
LAG = 5
LOW_LAG = 2
POOL_LOW_LAG = 1
POOL_LOW = (1, 5, 9)
OUT_LAG = 3


def score_chunks():
    out = []
    for half in range(2):
        for kt in range(4 * (half + 1)):
            q0 = max(HALF * half, P * kt)
            out.append((half, kt, q0, HALF * (half + 1) - q0))
    return out


def max_chunks():
    out = []
    for qt in range(8):
        for part in range(1 + qt // 4):
            k0 = HALF * part
            out.append((qt, part, k0, min(HALF, P * (qt + 1) - k0)))
    return out


CHUNKS = score_chunks()
MAXES = max_chunks()
NMAX = len(MAXES) + 1
assert len(CHUNKS) == NSTEP

MAX_AT = {7: [(2, 0), (2, 1)], 8: [(2, 2)], 9: [(2, 3)], 10: [(2, 4), (2, 5)], 11: [(2, 6)],
          0: [(1, 7)], 1: [(1, 8)], 2: [(1, 9)], 3: [(1, 10)], 4: [(1, 11)], 6: [(1, NMAX - 1)]}
NEARLY = 7
JOIN_AT = 5
LN_STATS_AT, LN_TURN_AT, LN_SPLIT_AT = 1, 5, 6
A_ITEMS = ["v0", "v1"] + [f"qk{m}" for m in range(8)]
A_AT = dict(zip([10, 14, 18, 22, 26, 30, 34, 38, 42, 46], A_ITEMS))
A_NTURN, A_NITEM = 2, len(A_ITEMS)
A_N = A_NTURN + A_NITEM


ATT_AT, ATT_SPLIT_AT, BASE_AT = 2, 3, 4
PROJECT_AT = (5, 6)
RESIDUAL_AT = (6, 7)
STATS_AT, RSTD_AT, NORM_AT, TURN_AT, REST_AT = 8, 9, 10, 11, 11
ROWS_HI_AT, ROWS_LO_AT = 12, 13
FINISH_AT = OUT_LAG - 1

PIECE_AT = {14: 0, 30: 1}
PIECE_LOW_AT = {17: (0, 0), 20: (0, 1), 33: (1, 0), 36: (1, 1)}


def low_place(c):
    mine = [k for k in range(NSTEP) if (k in POOL_LOW) == (c in POOL_LOW)]
    return ("prob_lo_pool" if c in POOL_LOW else "prob_lo"), len(mine), mine.index(c) + 1


def flat(i, s):
    j, c = divmod(s, NSTEP)
    return (i - 1, j + GH, c) if j < 0 else (i, j, c)


def wait(eng, sem, value):
    if isinstance(value, int) and value <= 0:
        return
    eng.wait_ge(sem, value)


def build(nc, x, cond, Wqkv, Wproj, bproj, W1, b1, W2, b2, g1, be1, g2, be2, Wada, bada, out):
    B, T, D = x.shape
    H, HD = 16, 32
    F = W1.shape[1]
    KT = D // P
    FT = F // P
    ROWS = B * T
    QK3 = 3 * D
    SCALE = float(HD) ** -0.5
    VW = 2 * HD + 1
    NIT = B * H // GH
    NA = ROWS // RA
    NR = RA // P
    IPB = H // GH
    assert NIT == NA == 32 and KT == 4 and NR == 2 and T == 1024 and IPB == 4

    x_rows = x.rearrange("b t d -> (b t) d")
    out_rows = out.rearrange("b t d -> (b t) d")
    qk_dram = nc.dram_tensor("qk_split", (2, IPB, 2, P, ROWS), F32, kind="Internal").ap()
    v_dram = nc.dram_tensor("v_split", (ROWS, H, VW), F32, kind="Internal").ap()
    o_dram = nc.dram_tensor("attended", (H, VW, ROWS), F32, kind="Internal").ap()
    r_dram = nc.dram_tensor("inverse_sums", (H, ROWS), F32, kind="Internal").ap()
    mod_dram = nc.dram_tensor("modulation", (6, B, D), F32, kind="Internal").ap()

    with ExitStack() as keep:
        sems = {}

        def sem(name):
            if name not in sems:
                sems[name] = keep.enter_context(nc.semaphore(name))
            return sems[name]

        def sb(stack, name, shape, dt=F32):
            return stack.enter_context(nc.sbuf_tensor(name, shape, dt))

        def sb_full_low(stack, name, shape):
            with nc.sbuf_tensor(name + "_full", shape, F32) as full:
                pass
            return full, sb(stack, name + "_l", shape, F32R)

        def psum(stack, name, shape):
            return stack.enter_context(nc.psum_tensor(name, shape, F32))

        ident = sb(keep, "ident", [P, P])
        coef = sb(keep, "coef", [P, 4, B, KT])
        b1c = sb(keep, "b1c", [P, FT])
        gb = sb(keep, "gb", [P, 4, KT])

        power = sb(keep, "power", [P, NR])

        att = ExitStack()
        wqkv_h = sb(att, "wqkv_h", [P, KT, QK3], F32R)
        wqkv, wqkv_l = sb_full_low(att, "wqkv", [P, KT, QK3])
        bada_sb = sb(att, "bada_sb", [B, 6, D])
        mod = sb(att, "mod", [B, 6, D])
        csb = sb(att, "csb", [B, 4, D])
        xin = sb(att, "xin", [P, NR, D])
        xn = sb(att, "xn", [P, NR, D])
        xm_h = sb(att, "xm_h", [P, KT, RA], F32R)
        xm, xm_l = sb_full_low(att, "xm", [P, KT, RA])
        ident_b = sb(att, "ident_b", [P, P], BF16)
        mask_q = sb(att, "mask_q", [P, P], BF16)
        mask_k = sb(att, "mask_k", [P, P], BF16)
        sT = sb(att, "sT", [P, KT, B])
        stats = sb(att, "stats", [P, NR, 6])
        aggr = sb(att, "aggr", [P, NR, 2])
        rstd = sb(att, "rstd", [P, NR])
        veps = sb(att, "veps", [P, NR])
        qk_h = sb(att, "qk_h", [P, 2, RA], F32R)
        qk_l = sb(att, "qk_l", [P, 2, RA], F32R)
        vaug = sb(att, "vaug", [P, NR, H, VW], F32R)
        with nc.sbuf_tensor("wada", [P, 6, KT, D], F32) as wada:
            pass
        qst = sb(att, "qst", [P, GH, T], F32R)
        e_h = sb(att, "e_h", [P, RING, HALF], F32R)
        e_full, e_l = sb_full_low(att, "e", [P, RING, HALF])
        kst = sb(att, "kst", [P, GH, T], F32R)
        vst = sb(att, "vst", [P, GH, T // P, VW], F32R)
        o_sb = sb(att, "o_sb", [VW, 2, HALF])
        mx = sb(att, "mx", [P, 2, 8])
        mxc = sb(att, "mxc", [P, 8])
        m_row = sb(att, "m_row", [8, 2, P], F32R)
        psS = psum(att, "psS", [P, 2, HALF])
        psT = psum(att, "psT", [P, 2, HALF])
        psO = psum(att, "psO", [P, 2, HALF])
        psA = psum(att, "psA", [P, 2, HALF])
        att.close()

        mlp = ExitStack()
        NP1 = (F + D) * KT // 1024
        wa_h = sb(mlp, "w1p_h", [P, NP1, 1024], F32R)
        wa, wa_l = sb_full_low(mlp, "w1p", [P, NP1, 1024])
        w1_h, w1_l = (t[:, 0:KT * F // 1024].rearrange("p a b -> p (a b)").rearrange("p (k f) -> p k f", k=KT)
                      for t in (wa_h, wa_l))
        wp_h, wp_l = (t[:, KT * F // 1024:NP1].rearrange("p a b -> p (a b)").rearrange("p (k d) -> p k d", k=KT)
                      for t in (wa_h, wa_l))
        w2_h = sb(mlp, "w2_h", [P, FT, D], F32R)
        w2_full, w2_l = sb_full_low(mlp, "w2", [P, FT, D])
        oin = sb(mlp, "oin", [P, 3, KT, RA])
        a_h = sb(mlp, "a_h", [P, 2, KT, RA], F32R)
        a_full, a_l = sb_full_low(mlp, "a", [P, 2, KT, RA])
        xc = sb(mlp, "xc", [P, NR, D])
        x1 = sb(mlp, "x1", [P, 2, NR, D])
        gate1 = sb(mlp, "gate1", [P, D])
        gate2 = sb(mlp, "gate2", [P, 2, D])
        bias1 = sb(mlp, "bias1", [P, 1, D])
        bias2 = sb(mlp, "bias2", [P, 1, D])
        tmp = sb(mlp, "tmp", [P, 2, D])
        h_h = sb(mlp, "h_h", [P, 4, RA], F32R)
        h_full, h_l = sb_full_low(mlp, "h", [P, 4, RA])
        stats2 = sb(mlp, "stats2", [P, NR, 6])
        aggr2 = sb(mlp, "aggr2", [P, NR, 2])
        rstd2 = sb(mlp, "rstd2", [P, NR])
        veps2 = sb(mlp, "veps2", [P, NR])
        psY = psum(mlp, "psY", [P, NR, D])
        psH = psum(mlp, "psH", [P, 4, D])
        psP = psum(mlp, "psP", [P, 2, D])
        mlp.close()

        qk_loaded = [sem(f"qk_loaded{j}") for j in range(GH)]
        v_loaded = [sem(f"v_loaded{j}") for j in range(GH)]
        m_loaded = [sem(f"m_loaded{j}") for j in range(GH)]
        qk_stored = [sem(f"qk_stored{j}") for j in range(2)]
        v_stored = [sem(f"v_stored{j}") for j in range(2)]
        o_stored = [sem(f"o_stored{j}") for j in range(2)]
        NQKL = 6 * 16

        w1_v = W1.rearrange("(k p) (h f) -> p k h f", p=P, h=2)
        w2_v = W2.rearrange("(k p) d -> p k d", p=P)
        wp_v = Wproj.rearrange("(k p) d -> p k d", p=P)
        wq_v = Wqkv.rearrange("(k p) n -> p k n", p=P)
        wa_v = Wada.rearrange("(k p) n -> p k n", p=P)
        W2_PIECES = FT // 2

        def w2_piece(t, n):
            return t[:, 2 * n:2 * n + 2, :]

        def past(eng, name):
            eng.sem_inc(sem(f"past_{name}"), 1)

        block = keep.enter_context(nc.Block())

        @block.sync
        def _(sp):
            sp.dma_start(csb[:, 0], cond).then_inc(sem("cond_loaded"), 16)
            sp.dma_start(bada_sb[:], bada.rearrange("(n d) -> n d", n=6).partition_broadcast(B))\
              .then_inc(sem("bada_loaded"), 16)
            for n, v in enumerate((g1, be1, g2, be2)):
                sp.dma_start(gb[:, n], v).then_inc(sem("small_loaded"), 16)
            sp.dma_start(b1c[:], b1).then_inc(sem("small_loaded"), 16)

            def load_x(ia):
                wait(sp, sem("xn_ready"), ia)
                sp.dma_start(xin[:], x_rows[bass.ds(ia * RA, RA)].rearrange("(r p) d -> p r d", p=P))\
                  .then_inc(sem("x_loaded"), 16)

            load_x(0)
            for n in range(6):
                sp.dma_start(wada[:, n], wa_v[:, :, n * D:(n + 1) * D]).then_inc(sem(f"wada_loaded{n}"), 16)
                if n == 1:
                    for k in range(KT):
                        sp.dma_start(wqkv[:, k], wq_v[:, k]).then_inc(sem(f"wqkv_loaded{k}"), 16)
            for half, (first, end) in enumerate(((0, 2), (2, 6))):
                sp.wait_ge(sem("mod_ready"), end)
                sp.dma_start(mod_dram[first:end].rearrange("n b d -> b n d"), mod[:, first:end])\
                  .then_inc(sem("mod_stored"), 16)
                if half == 0:
                    load_x(1)

            for ia in range(2, AHEAD + 1):
                load_x(ia)

            def load_head(i, j):
                b, hg = (i // IPB, i % IPB) if isinstance(i, int) else (i // IPB, i % IPB)
                done = (b + 1) * IPB
                if j == 0:
                    for s in range(2):
                        wait(sp, qk_stored[s], done * (4 * 32))
                        past(sp, "sp")
                        wait(sp, v_stored[s], done * 16)
                        past(sp, "sp")
                rows = bass.ds(b * T, T)
                wait(sp, sem("scores_ready"), i * (GH * NSTEP) - (GH - 1 - j) * NSTEP
                     if not isinstance(i, int) or i > 0 else 0)
                for tile, kind, order in ((kst, 1, (0, 1, 0)), (qst, 0, (0, 0, 1))):
                    for s, hl in enumerate(order):
                        sp.dma_start(tile[HD * s:HD * (s + 1), j, :].bitcast(F32),
                                     qk_dram[kind, hg, hl, HD * j:HD * (j + 1), rows]
                                     if isinstance(i, int) else
                                     qk_dram[kind, bass.ds(hg, 1), hl, HD * j:HD * (j + 1), rows]
                                     .rearrange("a p r -> (a p) r"))\
                          .then_inc(qk_loaded[j], 16)
                wait(sp, sem("pv_done"), i * (GH * NSTEP) - (GH - 1 - j) * NSTEP
                     if not isinstance(i, int) or i > 0 else 0)
                src = v_dram[rows].rearrange("(k p) h c -> p k h c", p=P)
                if isinstance(i, int):
                    src = src[:, :, hg * GH + j]
                else:
                    src = src[:, :, bass.ds(hg * GH + j, 1)].rearrange("p k h c -> p k (h c)")
                sp.dma_start(vst[:, j].bitcast(F32), src).then_inc(v_loaded[j], 16)

            def place_max(i, j):
                wait(sp, sem("max_done"), (i * GH + j + 1) * NMAX)
                sp.dma_start(qst[96:97, j, :].bitcast(F32), m_row[:, j % 2, :].bitcast(F32)).then_inc(m_loaded[j], 16)

            for j in range(GH):
                load_head(0, j)
            place_max(0, 0)

            def turn(i, with_x):
                for j in range(GH):
                    place_max(i - 1 if j < 3 else i, (j + 1) % GH)
                    load_head(i, j)
                    if j == 2 and with_x:
                        load_x(i + AHEAD)

            def load_piece(i):
                n = (i - (NIT - AHEAD)) * 2
                sp.wait_ge(sem("a_formed"), NA * A_N)
                wait(sp, sem("w1p_hi"), n)
                for q in range(2):
                    if isinstance(i, int) and i == NIT - 1:
                        src = wp_v[:, 2 * q:2 * q + 2]
                        dst = wa[:, n + q].rearrange("p (k d) -> p k d", k=2)
                    else:
                        src = w1_v[:, bass.ds(i - (NIT - AHEAD), 1), q].rearrange("p k f -> p (k f)")
                        dst = wa[:, bass.ds(n + q, 1)].rearrange("p a f -> p (a f)")
                    sp.dma_start(dst, src).then_inc(sem(f"w1p_loaded{q}"), 16)

            with sp.Fori(1, NIT - AHEAD) as i:
                turn(i, True)
            turn(NIT - AHEAD, False)
            load_piece(NIT - AHEAD)
            with sp.Fori(NIT - AHEAD + 1, NIT - 1) as i:
                turn(i, False)
                load_piece(i)
            turn(NIT - 1, False)
            load_piece(NIT - 1)
            for j in range(1, GH):
                place_max(NIT - 1, j)

            for s in range(2):
                sp.wait_ge(o_stored[s], 16 * NIT * GH)
            seg = 8
            for h in range(H):
                sp.dma_start(x1[seg * h:seg * (h + 1), 0].rearrange("p r d -> p (r d)"),
                             o_dram[h, 2 * HD].rearrange("(s r) -> s r", s=seg)).then_inc(sem("sums_loaded"), 16)

            def load_attended(u, parts=(0, 1, 2)):
                rows = bass.ds(u * RA, RA)
                wait(sp, sem("att_ready"), u)
                o_v = o_dram.rearrange("(k j) c r -> j c k r", j=GH)
                r_v = r_dram.rearrange("(k j) r -> j k r", j=GH)
                for j in range(GH):
                    for part in parts:
                        src = o_v[j, HD * part:HD * (part + 1), :, rows] if part < 2 else \
                            r_v[j, :, rows].partition_broadcast(HD)
                        sp.dma_start(oin[HD * j:HD * (j + 1), part], src).then_inc(sem("o_loaded"), 16)

            def load_gate(dst, m, u, done):
                b = u // IPB
                src = mod_dram[m, b] if isinstance(u, int) else \
                    mod_dram[m, bass.ds(b, 1)].rearrange("a d -> (a d)")
                sp.dma_start(dst, src.partition_broadcast(P)).then_inc(done, 16)

            def load_x_gate(u):
                wait(sp, sem("x1_based"), u)
                load_gate(gate1[:], 2, u, sem("gate1_loaded"))
                for dst, src in ((bias1[:, 0], bproj), (bias2[:, 0], b2)):
                    sp.dma_start(dst, src.partition_broadcast(P)).then_inc(sem("gate1_loaded"), 16)
                wait(sp, sem("turned2"), 2 * u)
                sp.dma_start(xc[:], x_rows[bass.ds(u * RA, RA)].rearrange("(r p) d -> p r d", p=P))\
                  .then_inc(sem("xc_loaded"), 16)

            def load_gate2(u, par):
                wait(sp, sem("y_added"), 2 * (u - 1) if not isinstance(u, int) or u > 0 else 0)
                load_gate(gate2[:, par], 5, u, sem("gate2_loaded"))

            def store_rows(u, par):
                sp.wait_ge(sem("y_added"), 2 * u + 2)
                sp.dma_start(out_rows[bass.ds(u * RA, RA)].rearrange("(r p) d -> p r d", p=P), x1[:, par])\
                  .then_inc(sem(f"out_stored{par}"), 16)

            def during(u, par, stores, loads):
                if stores:
                    store_rows(u - 1, 1 - par)
                load_gate2(u + 1, 1 - par)
                if loads:
                    load_attended(u + 2)
                    load_x_gate(u + 2)

            load_attended(0, (0, 1))
            sp.wait_ge(sem("mod_stored"), 32)
            load_x_gate(0)
            load_gate2(0, 0)
            sp.wait_ge(sem("sums_inverted"), 1)
            sp.dma_start(r_dram.rearrange("h (s r) -> (h s) r", s=seg), x1[:, 1].rearrange("p r d -> p (r d)"))\
              .then_inc(sem("inverses_stored"), 16)
            sp.wait_ge(sem("inverses_stored"), 16)
            load_attended(0, (2,))
            load_attended(1)
            load_x_gate(1)
            during(0, 0, False, True)
            during(1, 1, True, True)
            with sp.Fori(1, NA // 2 - 1) as uu:
                for par in range(2):
                    during(uu * 2 + par, par, True, True)
            during(NA - 2, 0, True, False)
            store_rows(NA - 2, 0)
            store_rows(NA - 1, 1)
            for par in range(2):
                sp.wait_ge(sem(f"out_stored{par}"), 16 * (NA // 2))

        @block.tensor
        def _(pe):
            pe.wait_ge(sem("ident_ready"), 2)
            pe.wait_ge(sem("silu_ready"), 1)
            for k in range(KT):
                mm = pe.transpose(psA[:, 0, k * B:(k + 1) * B], csb[:, 3, k * P:(k + 1) * P], ident[0:B, 0:B])
            mm.then_inc(sem("cond_turned"), 1)
            pe.wait_ge(sem("cond_copied"), 1)

            def modulation(first, end):
                for n in range(first, end + 1):
                    if n < end:
                        pe.wait_ge(sem(f"wada_loaded{n}"), 16)
                        wait(pe, sem("mod_ready"), n - 1)
                        for k in range(KT):
                            mm = pe.matmul(psT[0:B, n % 2, :], sT[:, k, :], wada[:, n, k, :],
                                           start=(k == 0), stop=(k == KT - 1))
                        mm.then_inc(sem("mod_formed"), 1)
                    if n > first:
                        pe.wait_ge(sem("mod_ready"), n)
                        for k in range(KT):
                            c = ((n - 1) * KT + k) * B
                            mm = pe.transpose(psO[:, int(n > 2), c:c + B], mod[:, n - 1, k * P:(k + 1) * P], ident[0:B, 0:B])
                        mm.then_inc(sem("mod_turned"), 1)

            modulation(0, 2)

            def part_a_turn(ia):
                pe.wait_ge(sem("xn_ready"), ia + 1)
                for n in range(A_NTURN):
                    wait(pe, sem("a_lo_done"), ia * A_NITEM - 1 + n if not isinstance(ia, int) or ia > 0 else 0)
                    for k in range(2):
                        for r in range(NR):
                            mm = pe.transpose(psA[:, n, k * RA + r * P:k * RA + (r + 1) * P],
                                              xn[:, r, (2 * n + k) * P:(2 * n + k + 1) * P], ident[:])
                    mm.then_inc(sem("a_formed"), 1)

            def part_a(ia, name):
                idx = A_NTURN + A_ITEMS.index(name)
                if idx == A_NTURN:
                    pe.wait_ge(sem("xm_hi"), ia + 1)
                    pe.wait_ge(sem("xm_lo"), ia + 1)
                if idx < 2 * A_NTURN:
                    pe.wait_ge(sem("a_hi_done"), ia * A_N + idx - 1)
                else:
                    pe.wait_ge(sem("a_lo_done"), ia * A_NITEM + idx - A_NTURN - 1)
                n = 0
                for k in range(KT):
                    if name[0] == "v":
                        r = int(name[1:])
                        for a, w in ((xm_h, wqkv_h), (xm_h, wqkv_l), (xm_l, wqkv_h)):
                            mm = pe.matmul(psA[:, idx % 2, :], a[:, k, r * P:(r + 1) * P], w[:, k, 2 * D:3 * D],
                                           start=(n == 0), stop=(n == 3 * KT - 1))
                            n += 1
                    else:
                        m = int(name[2:])
                        for a, w in ((xm_h, wqkv_h), (xm_l, wqkv_h), (xm_h, wqkv_l)):
                            mm = pe.matmul(psA[:, idx % 2, 0:RA], w[:, k, m * P:(m + 1) * P], a[:, k, :],
                                           start=(n == 0), stop=(n == 3 * KT - 1))
                            n += 1
                mm.then_inc(sem("a_formed"), 1)

            def max_item(i, j, n):
                head = i * GH + j
                if n == 0:
                    pe.wait_ge(qk_loaded[j], (i + 1) * NQKL)
                wait(pe, sem("max_done"), head * NMAX + n - 1)
                bank = psS[:, (j + n) % 2, :]
                if n == NMAX - 1:
                    pe.wait_ge(sem("max_joined"), head + 1)
                    pe.transpose(bank[0:8, 0:P], mxc[:], ident[:]).then_inc(sem("max_formed"), 1)
                    return
                qt, part, k0, w = MAXES[n]
                diag = k0 + w == P * (qt + 1)
                mm = pe.matmul(bank[:, 0:w], qst[0:96, j, qt * P:(qt + 1) * P], kst[0:96, j, k0:k0 + w],
                               start=True, stop=True)
                if diag:
                    mm = pe.matmul(bank[:, w - P:w], ident_b[:], mask_q[:], start=False, stop=True,
                                   skip_group_check=True)
                mm.then_inc(sem("max_formed"), 1)

            def scores(i, j, c):
                n = i * (GH * NSTEP) + j * NSTEP + c
                if c == 0:
                    pe.wait_ge(m_loaded[j], (i + 1) * 16)
                wait(pe, sem("exp_done"), n - 1)
                _, kt, q0, w = CHUNKS[c]
                bank = psT[:, c % 2, :]
                diag = q0 == P * kt
                mm = pe.matmul(bank[:, 0:w], kst[0:97, j, kt * P:(kt + 1) * P], qst[0:97, j, q0:q0 + w],
                               start=True, stop=True)
                if diag:
                    mm = pe.matmul(bank[:, 0:P], ident_b[:], mask_k[:], start=False, stop=True,
                                   skip_group_check=True)
                mm.then_inc(sem("scores_ready"), 1)

            def values(i, j, c):
                n = i * (GH * NSTEP) + j * NSTEP + c
                slot = (j * NSTEP + c) % RING
                half, kt, q0, w = CHUNKS[c]
                if c == 0:
                    pe.wait_ge(v_loaded[j], (i + 1) * 16)
                if kt == 0:
                    wait(pe, sem("o_copied"), (i * GH + j) * 2 + half - 1)
                pe.wait_ge(sem("prob_hi"), n + 1)
                lo, a_head, nth = low_place(c)
                pe.wait_ge(sem(lo), (i * GH + j) * a_head + nth)
                o = psO[0:VW, half, q0 - HALF * half:q0 - HALF * half + w]
                pe.matmul(o, vst[:, j, kt, :], e_h[:, slot, 0:w], start=(kt == 0), stop=True,
                          skip_group_check=True)
                pe.matmul(o, vst[:, j, kt, :], e_l[:, slot, 0:w], start=False, stop=True,
                          skip_group_check=True).then_inc(sem("pv_done"), 1)

            def iteration(i, with_a, last):
                for s in range(STEPS):
                    j, c = divmod(s, NSTEP)
                    scores(i, j, c)
                    for d, n in MAX_AT.get(c, ()):
                        if not (last and j + d >= GH):
                            max_item(i + (j + d) // GH, (j + d) % GH, n)
                    if with_a and s == LN_TURN_AT:
                        part_a_turn(i + AHEAD)
                    if with_a and s in A_AT:
                        part_a(i + AHEAD, A_AT[s])
                    if not (isinstance(i, int) and i == 0 and s < LAG):
                        values(*flat(i, s - LAG))

            pe.wait_ge(sem("wqkv_lo"), KT)
            part_a_turn(0)
            for name in A_ITEMS:
                part_a(0, name)
            modulation(2, 6)
            part_a_turn(1)
            with pe.Fori(1, AHEAD - 1) as ia:
                for name in A_ITEMS:
                    part_a(ia, name)
                part_a_turn(ia + 1)
            for name in A_ITEMS:
                part_a(AHEAD - 1, name)
            pe.wait_ge(sem("kst_set"), 1)
            pe.wait_ge(sem("masks_ready"), 2)
            for head, items in ((0, NMAX), (1, NEARLY)):
                for n in range(items):
                    max_item(0, head, n)
            iteration(0, True, False)
            with pe.Fori(1, NIT - AHEAD) as i:
                iteration(i, True, False)
            with pe.Fori(NIT - AHEAD, NIT - 1) as i:
                iteration(i, False, False)
            iteration(NIT - 1, False, True)
            for s in range(LAG):
                values(*flat(NIT, s - LAG))

            def project(u, par, r):
                pe.wait_ge(sem("att_lo"), u + 1)
                wait(pe, sem("y2_done"), 2 * (u - 1) + r + 1 if not isinstance(u, int) or u > 0 else 0)
                n = 0
                for k in range(KT):
                    for a, w in ((a_h, wp_h), (a_h, wp_l), (a_l, wp_h)):
                        mm = pe.matmul(psP[:, r, :], a[:, par, k, r * P:(r + 1) * P], w[:, k, :],
                                       start=(n == 0), stop=(n == 3 * KT - 1))
                        n += 1
                mm.then_inc(sem("projected"), 1)

            def turn2(u):
                pe.wait_ge(sem("xn2_ready"), u + 1)
                for n in range(2):
                    for k in range(2):
                        for r in range(NR):
                            mm = pe.transpose(psP[:, n, k * RA + r * P:k * RA + (r + 1) * P],
                                              xc[:, r, (2 * n + k) * P:(2 * n + k + 1) * P], ident[:])
                    mm.then_inc(sem("turned2"), 1)

            def hidden(u, par, m):
                if m == 0:
                    pe.wait_ge(sem("rows_lo"), u + 1)
                wait(pe, sem("gelu_done"), u * FT + m - 3)
                n = 0
                for k in range(KT):
                    for w, a in ((w1_h, a_h), (w1_h, a_l), (w1_l, a_h)):
                        mm = pe.matmul(psH[:, m % 4, 0:RA], w[:, k, m * P:(m + 1) * P], a[:, par, k, :],
                                       start=(n == 0), stop=(n == 3 * KT - 1))
                        n += 1
                mm.then_inc(sem("hidden_ready"), 1)

            def mlp_out(u, m):
                if isinstance(u, int) and u == 0 and m % 2 == 0:
                    pe.wait_ge(sem("w2_lo"), m // 2 + 1)
                pe.wait_ge(sem("h_lo"), u * FT + m + 1)
                for r in range(NR):
                    if m == 0:
                        wait(pe, sem("gated2"), 2 * u - 1 + r if not isinstance(u, int) or u > 0 else 0)
                    for n, (a, w) in enumerate(((h_h, w2_h), (h_h, w2_l), (h_l, w2_h))):
                        mm = pe.matmul(psY[:, r, :], a[:, m % 4, r * P:(r + 1) * P], w[:, m, :],
                                       start=(m == 0 and n == 0), stop=(m == FT - 1 and n == 2),
                                       skip_group_check=True)
                mm.then_inc(sem("mlp_done"), 1)

            def rows(u, par, prepare):
                for m in range(FT):
                    hidden(u, par, m)
                    if prepare:
                        if m in PROJECT_AT:
                            project(u + 1, 1 - par, PROJECT_AT.index(m))
                        if m == TURN_AT:
                            turn2(u + 1)
                    if m >= OUT_LAG:
                        mlp_out(u, m - OUT_LAG)
                    elif not (isinstance(u, int) and u == 0):
                        mlp_out(u - 1, FT + m - OUT_LAG)

            pe.wait_ge(sem("w1p_lo"), 2 * NP1)
            for r in range(NR):
                project(0, 0, r)
            turn2(0)
            for par in range(2):
                rows(par, par, True)
            with pe.Fori(1, NA // 2 - 1) as uu:
                for par in range(2):
                    rows(uu * 2 + par, par, True)
            rows(NA - 2, 0, True)
            rows(NA - 1, 1, False)
            for m in range(FT - OUT_LAG, FT):
                mlp_out(NA - 1, m)

        @block.scalar
        def _(act):
            act.wait_ge(sem("cond_loaded"), 16)
            act.activation(csb[:, 1], csb[:, 0], ACT.Exp, scale=-1.0).then_inc(sem("cond_exp"), 1)
            act.wait_ge(sem("cond_turned"), 1)
            act.activation(sT[:].rearrange("p k b -> p (k b)"), psA[:, 0, 0:KT * B], ACT.Copy)\
               .then_inc(sem("cond_copied"), 1)

            def a_modulate(ia):
                b = ia // IPB
                for n in range(A_NTURN):
                    act.wait_ge(sem("a_formed"), ia * A_N + n + 1)
                    for k in range(2):
                        kk = 2 * n + k
                        ca, cb = (coef[:, w, b, kk:kk + 1] if isinstance(ia, int) else
                                  coef[:, w, bass.ds(b, 1), kk] for w in (0, 1))
                        a = act.activation(xm[:, kk, :], psA[:, n, k * RA:(k + 1) * RA], ACT.Identity,
                                           scale=ca, bias=cb)
                    a.then_inc(sem("a_hi_done"), 1)

            def a_high(ia, name):
                idx = A_NTURN + A_ITEMS.index(name)
                if name[0] == "v":
                    r = int(name[1:])
                    wait(act, v_stored[r], ia * 16)
                    dst = vaug[:, r, :, 0:HD]
                    src = psA[:, idx % 2, :].rearrange("p (h c) -> p h c", c=HD)
                else:
                    m = int(name[2:])
                    wait(act, qk_stored[m % 2], ia * (4 * 32) + (m // 2) * 32)
                    dst, src = qk_h[:, m % 2, :], psA[:, idx % 2, 0:RA]
                act.wait_ge(sem("a_formed"), ia * A_N + idx + 1)
                act.activation(dst, src, ACT.Copy).then_inc(sem("a_hi_done"), 1)

            def a_store(ia, name):
                idx = A_ITEMS.index(name)
                act.wait_ge(sem("a_hi_done"), ia * A_N + A_NTURN + idx + 1)
                act.wait_ge(sem("a_lo_done"), ia * A_NITEM + idx + 1)
                if name[0] == "v":
                    r = int(name[1:])
                    act.dma_start(v_dram[bass.ds(ia * RA + r * P, P)].rearrange("p h c -> p (h c)"),
                                  vaug[:, r].rearrange("p h c -> p (h c)").bitcast(F32)).then_inc(v_stored[r], 16)
                else:
                    m = int(name[2:])
                    for hl, t in enumerate((qk_h, qk_l)):
                        act.dma_start(qk_dram[m // IPB, m % IPB, hl, :, bass.ds(ia * RA, RA)], t[:, m % 2, :].bitcast(F32))\
                           .then_inc(qk_stored[m % 2], 16)

            def part_a(ia, name):
                a_high(ia, name)
                at = A_ITEMS.index(name)
                if at:
                    a_store(ia, A_ITEMS[at - 1])

            def exps(i, j, c):
                n = i * (GH * NSTEP) + j * NSTEP + c
                slot = (j * NSTEP + c) % RING
                w = CHUNKS[c][3]
                wait(act, sem("pv_done"), n - RING + 1)
                act.wait_ge(sem("scores_ready"), n + 1)
                act.activation(e_full[:, slot, 0:w], psT[:, c % 2, 0:w], ACT.Exp, scale=SCALE)\
                   .then_inc(sem("exp_done"), 1)

            def o_copy(i, j, half):
                head = i * GH + j
                wait(act, o_stored[half], head * 16)
                act.wait_ge(sem("pv_done"), head * NSTEP + (4 if half == 0 else NSTEP))
                act.activation(o_sb[:, half, :], psO[0:VW, half, :], ACT.Copy).then_inc(sem("o_copied"), 1)

            def o_store(i, j, half):
                act.wait_ge(sem("o_copied"), (i * GH + j) * 2 + half + 1)
                b, hg = i // IPB, i % IPB
                cols = bass.ds(b * T + half * HALF, HALF)
                dst = o_dram[hg * GH + j, :, cols] if isinstance(i, int) else \
                    o_dram[bass.ds(hg * GH + j, 1), :, cols].rearrange("a c r -> (a c) r")
                act.dma_start(dst, o_sb[:, half, :]).then_inc(o_stored[half], 16)

            def outputs(i, s):
                for half, end in ((0, 4), (1, NSTEP)):
                    for lag, what in ((0, o_copy), (1, o_store)):
                        at = s - end - LAG - lag
                        if at % NSTEP == 0 and not (isinstance(i, int) and i == 0 and at < 0):
                            ii, j, _ = flat(i, at)
                            what(ii, j, half)

            def piece_high(i, q):
                n = (i - (NIT - AHEAD)) * 2 + q
                act.wait_ge(sem(f"w1p_loaded{q}"), (i - (NIT - AHEAD) + 1) * 16)
                act.activation(wa_h[:, bass.ds(n, 1)], wa[:, bass.ds(n, 1)], ACT.Copy)\
                   .then_inc(sem("w1p_hi"), 1)

            def iteration(i, with_a):
                for s in range(STEPS):
                    outputs(i, s)
                    exps(i, *divmod(s, NSTEP))
                    if with_a and s == LN_TURN_AT:
                        a_modulate(i + AHEAD)
                    if with_a and s in A_AT:
                        part_a(i + AHEAD, A_AT[s])
                    if not with_a and s in PIECE_AT:
                        piece_high(i, PIECE_AT[s])
                if with_a:
                    a_store(i + AHEAD, A_ITEMS[-1])

            def a_products(ia):
                for name in A_ITEMS:
                    part_a(ia, name)
                a_store(ia, A_ITEMS[-1])

            for k in range(KT):
                act.wait_ge(sem(f"wqkv_loaded{k}"), 16)
                act.activation(wqkv_h[:, k, :], wqkv[:, k, :], ACT.Copy).then_inc(sem("wqkv_hi"), 1)
            act.wait_ge(sem("coef_ready"), 1)
            a_modulate(0)
            a_products(0)
            a_modulate(1)
            with act.Fori(1, AHEAD - 1) as ia:
                a_products(ia)
                a_modulate(ia + 1)
            a_products(AHEAD - 1)
            iteration(0, True)
            with act.Fori(1, NIT - AHEAD) as i:
                iteration(i, True)
            with act.Fori(NIT - AHEAD, NIT) as i:
                iteration(i, False)
            for s in range(LAG + 2):
                outputs(NIT, s)

            for half in range(2):
                act.wait_ge(o_stored[half], 16 * NIT * GH)
            for n in range(W2_PIECES):
                act.dma_start(w2_piece(w2_full, n), w2_piece(w2_v, n)).then_inc(sem(f"w2_loaded{n}"), 16)

            def modulate2(u, par):
                b = u // IPB
                for n in range(2):
                    act.wait_ge(sem("turned2"), 2 * u + n + 1)
                    for k in range(2):
                        kk = 2 * n + k
                        ca, cb = (coef[:, w, b, kk:kk + 1] if isinstance(u, int) else
                                  coef[:, w, bass.ds(b, 1), kk] for w in (2, 3))
                        a = act.activation(a_full[:, par, kk, :], psP[:, n, k * RA:(k + 1) * RA],
                                           ACT.Identity, scale=ca, bias=cb)
                    a.then_inc(sem("y2_done"), 1)

            def gelu(u, m):
                wait(act, sem("mlp_done"), u * FT + m - 3)
                act.wait_ge(sem("hidden_ready"), u * FT + m + 1)
                act.activation(h_full[:, m % 4, :], psH[:, m % 4, 0:RA], ACT.Gelu, bias=b1c[:, m:m + 1])\
                   .then_inc(sem("gelu_done"), 1)

            def rows(u, par, prepare):
                for m in range(FT):
                    gelu(u, m)
                    if prepare and m == TURN_AT:
                        modulate2(u + 1, 1 - par)

            act.wait_ge(sem("small_loaded"), 5 * 16)
            modulate2(0, 0)
            for par in range(2):
                rows(par, par, True)
            with act.Fori(1, NA // 2 - 1) as uu:
                for par in range(2):
                    rows(uu * 2 + par, par, True)
            rows(NA - 2, 0, True)
            rows(NA - 1, 1, False)

        @block.vector
        def _(dve):
            dve.memset(mx[:], LOWEST).then_inc(sem("mx_set"), 1)
            dve.memset(kst[96:97].bitcast(F32), -1.0).then_inc(sem("kst_set"), 1)
            dve.wait_ge(sem("cond_exp"), 1)
            dve.tensor_scalar_add(csb[:, 1], csb[:, 1], 1.0).then_inc(sem("silu_step"), 1)
            dve.wait_ge(sem("silu_step"), 1)
            dve.reciprocal(csb[:, 2], csb[:, 1]).then_inc(sem("silu_step"), 1)
            dve.wait_ge(sem("silu_step"), 2)
            dve.tensor_tensor(csb[:, 3], csb[:, 0], csb[:, 2], ALU.mult).then_inc(sem("silu_ready"), 1)

            def wqkv_low(k):
                dve.wait_ge(sem("wqkv_hi"), k + 1)
                dve.tensor_tensor(wqkv_l[:, k, :], wqkv[:, k, :], wqkv_h[:, k, :].bitcast(F32),
                                  ALU.subtract).then_inc(sem("wqkv_lo"), 1)

            dve.wait_ge(sem("bada_loaded"), 16)

            def modulation(first, end):
                for n in range(first, end):
                    dve.wait_ge(sem("mod_formed"), n + 1)
                    dve.tensor_tensor(mod[:, n], psT[0:B, n % 2, :], bada_sb[:, n], ALU.add)\
                       .then_inc(sem("mod_ready"), 1)

            def coefficients(c, shift, scale):
                dve.wait_ge(sem("mod_turned"), 2 + 4 * c)
                turned = psO[:, c, 0:6 * KT * B].rearrange("p (n k b) -> p n k b", n=6, k=KT)
                for k in range(KT):
                    for w in range(2):
                        dve.tensor_scalar(coef[:, 2 * c + w, :, k], turned[:, scale, k, :], 1.0,
                                          gb[:, 2 * c + w, k:k + 1], ALU.add, ALU.mult).then_inc(sem("coef_step"), 1)
                dve.wait_ge(sem("coef_step"), 2 * KT * (c + 1))
                dve.tensor_tensor(coef[:, 2 * c + 1].rearrange("p b k -> p k b"),
                                  coef[:, 2 * c + 1].rearrange("p b k -> p k b"), turned[:, shift], ALU.add)\
                   .then_inc(sem("coef_ready"), 1)

            modulation(0, 2)
            dve.wait_ge(sem("small_loaded"), 5 * 16)
            coefficients(0, 0, 1)
            for k in range(KT):
                wqkv_low(k)

            def normalise(ia):
                dve.wait_ge(sem("x_loaded"), 16 * (ia + 1))
                for r in range(NR):
                    dve.bn_stats(stats[:, r], xin[:, r]).then_inc(sem("ln_stats"), 1)
                for r in range(NR):
                    dve.wait_ge(sem("ln_stats"), ia * NR + r + 1)
                    past(dve, "dve")
                    dve.bn_aggr(aggr[:, r], stats[:, r]).then_inc(sem("ln_aggr"), 1)
                dve.wait_ge(sem("ln_aggr"), ia * NR + NR)
                dve.tensor_scalar_add(veps[:], aggr[:, :, 1], EPS).then_inc(sem("ln_veps"), 1)
                dve.wait_ge(sem("ln_rstd"), ia + 1)
                wait(dve, sem("a_formed"), ia * A_N - A_NITEM if not isinstance(ia, int) or ia > 0 else 0)
                for r in range(NR):
                    a = dve.tensor_scalar(xn[:, r], xin[:, r], aggr[:, r, 0:1], rstd[:, r:r + 1],
                                          ALU.subtract, ALU.mult)
                a.then_inc(sem("xn_ready"), 1)

            def a_split(ia):
                dve.wait_ge(sem("a_hi_done"), ia * A_N + A_NTURN)
                wait(dve, sem("a_formed"), ia * A_N)
                dve.tensor_copy(xm_h[:], xm[:]).then_inc(sem("xm_hi"), 1)

            def a_low(ia, name):
                idx = A_NTURN + A_ITEMS.index(name)
                dve.wait_ge(sem("a_hi_done"), ia * A_N + idx + 1)
                if name[0] == "v":
                    r = int(name[1:])
                    src = psA[:, idx % 2, :].rearrange("p (h c) -> p h c", c=HD)
                    hi, lo = vaug[:, r, :, 0:HD], vaug[:, r, :, HD:2 * HD]
                else:
                    m = int(name[2:])
                    src, hi, lo = psA[:, idx % 2, 0:RA], qk_h[:, m % 2, :], qk_l[:, m % 2, :]
                dve.tensor_tensor(lo, src, hi.bitcast(F32), ALU.subtract).then_inc(sem("a_lo_done"), 1)

            def max_item(i, j, n):
                head = i * GH + j
                if n == NMAX - 1:
                    slot = (j - 2) % GH
                    wait(dve, m_loaded[slot], (i + (j - 2) // GH + 1) * 16)
                    dve.wait_ge(sem("max_formed"), head * NMAX + n + 1)
                    dve.tensor_copy(m_row[:, j % 2, :], psS[0:8, (j + n) % 2, 0:P]).then_inc(sem("max_done"), 1)
                    return
                qt, part, _, w = MAXES[n]
                if n == 0:
                    wait(dve, sem("max_joined"), head)
                dve.wait_ge(sem("max_formed"), head * NMAX + n + 1)
                dve.tensor_reduce(mx[:, part, qt:qt + 1], psS[:, (j + n) % 2, 0:w], AX_X, ALU.max)\
                   .then_inc(sem("max_done"), 1)

            def max_join(i, j):
                head = i * GH + j
                dve.wait_ge(sem("max_done"), head * NMAX + NMAX - 1)
                wait(dve, sem("max_done"), head * NMAX)
                dve.tensor_tensor(mxc[:], mx[:, 0], mx[:, 1], ALU.max).then_inc(sem("max_joined"), 1)

            def prob_low(i, j, c):
                n = i * (GH * NSTEP) + j * NSTEP + c
                slot = (j * NSTEP + c) % RING
                w = CHUNKS[c][3]
                dve.wait_ge(sem("prob_hi"), n + 1)
                dve.tensor_tensor(e_l[:, slot, 0:w], e_full[:, slot, 0:w], e_h[:, slot, 0:w].bitcast(F32),
                                  ALU.subtract).then_inc(sem("prob_lo"), 1)

            def low_step(i, s):
                if isinstance(i, int) and i == 0 and s < LOW_LAG:
                    return
                at = flat(i, s - LOW_LAG)
                if at[2] not in POOL_LOW:
                    prob_low(*at)

            def iteration(i, with_a, last):
                for s in range(STEPS):
                    j, c = divmod(s, NSTEP)
                    for d, n in MAX_AT.get(c, ()):
                        if not (last and j + d >= GH):
                            max_item(i + (j + d) // GH, (j + d) % GH, n)
                    if c == JOIN_AT and not (last and j + 1 >= GH):
                        max_join(i + (j + 1) // GH, (j + 1) % GH)
                    if with_a and s == LN_STATS_AT:
                        normalise(i + AHEAD)
                    if with_a and s == LN_SPLIT_AT:
                        a_split(i + AHEAD)
                    low_step(i, s)
                    if with_a and s in A_AT:
                        a_low(i + AHEAD, A_AT[s])

            normalise(0)
            a_split(0)
            dve.wait_ge(sem("ones_set"), 2)
            for name in A_ITEMS:
                if name == A_ITEMS[3]:
                    normalise(1)
                a_low(0, name)
            modulation(2, 6)
            coefficients(1, 3, 4)
            a_split(1)
            with dve.Fori(1, AHEAD - 1) as ia:
                for name in A_ITEMS:
                    if name == A_ITEMS[3]:
                        normalise(ia + 1)
                    a_low(ia, name)
                a_split(ia + 1)
            for name in A_ITEMS:
                a_low(AHEAD - 1, name)
            dve.wait_ge(sem("mx_set"), 1)
            for head, items in ((0, NMAX), (1, NEARLY)):
                for n in range(items):
                    if n == NMAX - 1:
                        max_join(0, head)
                    max_item(0, head, n)
            iteration(0, True, False)
            with dve.Fori(1, NIT - AHEAD) as i:
                iteration(i, True, False)
            with dve.Fori(NIT - AHEAD, NIT - 1) as i:
                iteration(i, False, False)
            iteration(NIT - 1, False, True)
            for s in range(LOW_LAG):
                low_step(NIT, s)

            dve.wait_ge(sem("sums_loaded"), 16 * H)
            dve.reciprocal(x1[:, 1], x1[:, 0]).then_inc(sem("sums_inverted"), 1)

            def attended(u, par):
                dve.wait_ge(sem("o_loaded"), 12 * 16 * (u + 1))
                dve.tensor_tensor(oin[:, 0], oin[:, 0], oin[:, 1], ALU.add).then_inc(sem("att_joined"), 1)
                dve.wait_ge(sem("att_joined"), u + 1)
                wait(dve, sem("hidden_ready"), (u - 1) * FT if not isinstance(u, int) or u > 1 else 0)
                dve.tensor_tensor(a_full[:, par], oin[:, 0], oin[:, 2], ALU.mult)\
                   .then_inc(sem("att_ready"), 1)

            def attended_split(u, par):
                dve.wait_ge(sem("att_ready"), u + 1)
                dve.tensor_copy(a_h[:, par], a_full[:, par]).then_inc(sem("att_hi"), 1)
                dve.wait_ge(sem("att_hi"), u + 1)
                dve.tensor_tensor(a_l[:, par], a_full[:, par], a_h[:, par].bitcast(F32), ALU.subtract)\
                   .then_inc(sem("att_lo"), 1)

            def base(u):
                dve.wait_ge(sem("gate1_loaded"), 48 * (u + 1))
                dve.tensor_tensor(bias1[:, 0], bias1[:, 0], gate1[:], ALU.mult).then_inc(sem("bias1_ready"), 1)
                dve.wait_ge(sem("bias1_ready"), u + 1)
                dve.wait_ge(sem("xc_loaded"), 16 * (u + 1))
                dve.tensor_tensor(xc[:], xc[:], bias1[:].to_broadcast([P, NR, D]), ALU.add)\
                   .then_inc(sem("xc_based"), 1)

            def residual(u, par, r):
                dve.wait_ge(sem("projected"), u * NR + r + 1)
                wait(dve, sem("y_added"), 2 * (u - 1) + r - 1)
                dve.tensor_tensor(tmp[:, r], psP[:, r], gate1[:], ALU.mult).then_inc(sem("gated"), 1)
                dve.wait_ge(sem("gated"), u * NR + r + 1)
                if r == 0:
                    dve.wait_ge(sem("xc_based"), u + 1)
                    wait(dve, sem(f"out_stored{par}"), (u // 2) * 16 if isinstance(u, int) else u * 8 - 8 * par)
                dve.tensor_tensor(x1[:, par, r], xc[:, r], tmp[:, r], ALU.add).then_inc(sem("x1_step"), 1)

            def statistics(u, par):
                for r in range(NR):
                    dve.wait_ge(sem("x1_step"), u * NR + r + 1)
                    dve.bn_stats(stats2[:, r], x1[:, par, r]).then_inc(sem("ln2_stats"), 1)

            def deviation(u):
                for r in range(NR):
                    dve.wait_ge(sem("ln2_stats"), u * NR + r + 1)
                    past(dve, "dve")
                    dve.bn_aggr(aggr2[:, r], stats2[:, r]).then_inc(sem("ln2_aggr"), 1)
                dve.wait_ge(sem("ln2_aggr"), u * NR + NR)
                dve.tensor_scalar_add(veps2[:], aggr2[:, :, 1], EPS).then_inc(sem("ln2_veps"), 1)

            def norm(u, par):
                dve.wait_ge(sem("ln2_rstd"), u + 1)
                for r in range(NR):
                    a = dve.tensor_scalar(xc[:, r], x1[:, par, r], aggr2[:, r, 0:1], rstd2[:, r:r + 1],
                                          ALU.subtract, ALU.mult)
                a.then_inc(sem("xn2_ready"), 1)

            def rest(u, par):
                dve.wait_ge(sem("gate2_loaded"), 16 * (u + 1))
                dve.tensor_tensor(bias2[:, 0], bias2[:, 0], gate2[:, par], ALU.mult).then_inc(sem("bias2_ready"), 1)
                dve.wait_ge(sem("bias2_ready"), u + 1)
                dve.wait_ge(sem("xn2_ready"), u + 1)
                dve.tensor_tensor(x1[:, par], x1[:, par], bias2[:].to_broadcast([P, NR, D]), ALU.add)\
                   .then_inc(sem("x1_based"), 1)

            def rows_high(u, par):
                dve.wait_ge(sem("y2_done"), 2 * u + 2)
                dve.tensor_copy(a_h[:, par], a_full[:, par]).then_inc(sem("rows_hi"), 1)

            def rows_low(u, par):
                dve.wait_ge(sem("rows_hi"), u + 1)
                dve.tensor_tensor(a_l[:, par], a_full[:, par], a_h[:, par].bitcast(F32), ALU.subtract)\
                   .then_inc(sem("rows_lo"), 1)

            def hidden_high(u, m):
                dve.wait_ge(sem("gelu_done"), u * FT + m + 1)
                dve.tensor_copy(h_h[:, m % 4, :], h_full[:, m % 4, :]).then_inc(sem("h_hi"), 1)

            def finish(u, par):
                dve.wait_ge(sem("mlp_done"), (u + 1) * FT)
                for r in range(NR):
                    wait(dve, sem("x1_step"), u * NR + r + 1)
                    dve.tensor_tensor(tmp[:, r], psY[:, r], gate2[:, par], ALU.mult).then_inc(sem("gated2"), 1)
                for r in range(NR):
                    dve.wait_ge(sem("gated2"), u * NR + r + 1)
                    if r == 0:
                        dve.wait_ge(sem("x1_based"), u + 1)
                    dve.tensor_tensor(x1[:, par, r], x1[:, par, r], tmp[:, r], ALU.add).then_inc(sem("y_added"), 1)

            def prepare_step(u, par, m):
                if m == ATT_AT:
                    attended(u, par)
                if m == ATT_SPLIT_AT:
                    attended_split(u, par)
                if m == BASE_AT:
                    base(u)
                if m in RESIDUAL_AT:
                    residual(u, par, RESIDUAL_AT.index(m))
                if m == STATS_AT:
                    statistics(u, par)
                if m == RSTD_AT:
                    deviation(u)
                if m == NORM_AT:
                    norm(u, par)
                if m == REST_AT:
                    rest(u, par)
                if m == ROWS_HI_AT:
                    rows_high(u, par)
                if m == ROWS_LO_AT:
                    rows_low(u, par)

            def rows(u, par, prepare):
                for m in range(FT):
                    hidden_high(u, m)
                    if m == FINISH_AT and not (isinstance(u, int) and u == 0):
                        finish(u - 1, 1 - par)
                    if prepare:
                        prepare_step(u + 1, 1 - par, m)

            for m in range(FT):
                prepare_step(0, 0, m)
            for par in range(2):
                rows(par, par, True)
            with dve.Fori(1, NA // 2 - 1) as uu:
                for par in range(2):
                    rows(uu * 2 + par, par, True)
            rows(NA - 2, 0, True)
            rows(NA - 1, 1, False)
            finish(NA - 1, 1)

        @block.gpsimd
        def _(pool):
            pool.memset(ident[:], 0.0).then_inc(sem("pool_set"), 1)
            pool.memset(ident_b[:], 0.0).then_inc(sem("pool_set"), 1)
            pool.memset(mask_q[:], 0.0).then_inc(sem("pool_set"), 1)
            pool.memset(mask_k[:], 0.0).then_inc(sem("pool_set"), 1)
            pool.memset(power[:], -0.5).then_inc(sem("pool_set"), 1)
            pool.wait_ge(sem("pool_set"), 5)
            pool.affine_select(out=ident[:], in_=ident[:], compare_op=ALU.not_equal, fill=1.0, base=0,
                               pattern=[[-1, P]], channel_multiplier=1).then_inc(sem("ident_ready"), 1)
            pool.affine_select(out=ident_b[:], in_=ident_b[:], compare_op=ALU.not_equal, fill=1.0, base=0,
                               pattern=[[-1, P]], channel_multiplier=1).then_inc(sem("ident_ready"), 1)
            for r in range(NR):
                pool.memset(vaug[:, r, :, 2 * HD:VW].bitcast(F32), 1.0).then_inc(sem("ones_set"), 1)
            pool.affine_select(out=mask_q[:], in_=mask_q[:], compare_op=ALU.is_ge, fill=MASKED, base=0,
                               pattern=[[-1, P]], channel_multiplier=1).then_inc(sem("masks_ready"), 1)
            pool.affine_select(out=mask_k[:], in_=mask_k[:], compare_op=ALU.is_ge, fill=MASKED, base=0,
                               pattern=[[1, P]], channel_multiplier=-1).then_inc(sem("masks_ready"), 1)

            def low(dst, full, high):
                return pool.tensor_tensor(dst, full, high.bitcast(F32), ALU.subtract)

            def a_rstd(ia):
                pool.wait_ge(sem("ln_veps"), ia + 1)
                pool.tensor_tensor(rstd[:], veps[:], power[:], ALU.pow).then_inc(sem("ln_rstd"), 1)

            def a_split(ia):
                pool.wait_ge(sem("xm_hi"), ia + 1)
                low(xm_l[:], xm[:], xm_h[:]).then_inc(sem("xm_lo"), 1)

            def prob_high(i, j, c):
                n = i * (GH * NSTEP) + j * NSTEP + c
                slot = (j * NSTEP + c) % RING
                w = CHUNKS[c][3]
                pool.wait_ge(sem("exp_done"), n + 1)
                past(pool, "pool")
                pool.tensor_scalar(e_h[:, slot, 0:w], e_full[:, slot, 0:w], 1.0, 1.0, ALU.mult, ALU.mult)\
                    .then_inc(sem("prob_hi"), 1)

            def low_step(i, s):
                if isinstance(i, int) and i == 0 and s < POOL_LOW_LAG:
                    return
                i, j, c = flat(i, s - POOL_LOW_LAG)
                if c in POOL_LOW:
                    slot = (j * NSTEP + c) % RING
                    w = CHUNKS[c][3]
                    pool.wait_ge(sem("prob_hi"), i * (GH * NSTEP) + j * NSTEP + c + 1)
                    low(e_l[:, slot, 0:w], e_full[:, slot, 0:w], e_h[:, slot, 0:w]).then_inc(sem("prob_lo_pool"), 1)

            def piece_low(i, q, part):
                n = (i - (NIT - AHEAD)) * 2 + q
                cols = slice(part * 512, (part + 1) * 512)
                pool.wait_ge(sem("w1p_hi"), n + 1)
                low(wa_l[:, bass.ds(n, 1), cols], wa[:, bass.ds(n, 1), cols], wa_h[:, bass.ds(n, 1), cols]).then_inc(sem("w1p_lo"), 1)

            def iteration(i, with_a):
                for s in range(STEPS):
                    prob_high(i, *divmod(s, NSTEP))
                    low_step(i, s)
                    if with_a and s == LN_STATS_AT:
                        a_rstd(i + AHEAD)
                    if with_a and s == LN_SPLIT_AT:
                        a_split(i + AHEAD)
                    if not with_a and s in PIECE_LOW_AT:
                        piece_low(i, *PIECE_LOW_AT[s])

            a_rstd(0)
            a_split(0)
            with pool.Fori(1, AHEAD) as ia:
                a_rstd(ia)
                a_split(ia)
            iteration(0, True)
            with pool.Fori(1, NIT - AHEAD) as i:
                iteration(i, True)
            with pool.Fori(NIT - AHEAD, NIT) as i:
                iteration(i, False)
            for s in range(POOL_LOW_LAG):
                low_step(NIT, s)

            def w2_split(n):
                pool.wait_ge(sem(f"w2_loaded{n}"), 16)
                pool.tensor_scalar(w2_piece(w2_h, n), w2_piece(w2_full, n), 1.0, 1.0, ALU.mult, ALU.mult)\
                    .then_inc(sem("w2_hi"), 1)
                pool.wait_ge(sem("w2_hi"), n + 1)
                low(w2_piece(w2_l, n), w2_piece(w2_full, n), w2_piece(w2_h, n)).then_inc(sem("w2_lo"), 1)

            def rstd_2(u):
                pool.wait_ge(sem("ln2_veps"), u + 1)
                pool.tensor_tensor(rstd2[:], veps2[:], power[:], ALU.pow).then_inc(sem("ln2_rstd"), 1)

            def hidden_low(u, m):
                pool.wait_ge(sem("h_hi"), u * FT + m + 1)
                low(h_l[:, m % 4, :], h_full[:, m % 4, :], h_h[:, m % 4, :]).then_inc(sem("h_lo"), 1)

            def rows(u, prepare):
                for m in range(FT):
                    hidden_low(u, m)
                    if prepare and m == RSTD_AT:
                        rstd_2(u + 1)

            for n in range(W2_PIECES // 2):
                w2_split(n)
            rstd_2(0)
            for n in range(W2_PIECES // 2, W2_PIECES):
                w2_split(n)
            rows(0, True)
            with pool.Fori(1, NA - 1) as u:
                rows(u, True)
            rows(NA - 1, False)


_INS = ['x', 'cond_1024', 'L0_cond_Wqkv', 'L0_cond_Wproj', 'L0_cond_bproj', 'L0_cond_W1', 'L0_cond_b1',
        'L0_cond_W2', 'L0_cond_b2', 'L0_cond_g1', 'L0_cond_be1', 'L0_cond_g2', 'L0_cond_be2', 'L0_cond_Wada',
        'L0_cond_bada']
_BY_PARTITION = ['L0_cond_b1', 'L0_cond_g1', 'L0_cond_be1', 'L0_cond_g2', 'L0_cond_be2']
_OUTS = [((8, 1024, 512), 'float32')]


def kernel(**inputs):
    import numpy as _np
    import concourse.bacc as _bacc
    from concourse import mybir as _mybir
    from concourse.bass_utils import run_bass_kernel_spmd as _run

    nc = _bacc.Bacc("TRN2", target_bir_lowering=False, num_devices=1)
    arrays, args = {}, []
    for name in _INS:
        a = _np.ascontiguousarray(inputs[name])
        if name in _BY_PARTITION:
            a = _np.ascontiguousarray(a.reshape(-1, P).T)
        arrays[f"in_{name}_dram"] = a
        args.append(nc.dram_tensor(f"in_{name}_dram", a.shape, _mybir.dt.from_np(a.dtype), kind="ExternalInput").ap())
    for i, (shape, dtype) in enumerate(_OUTS):
        dt = _mybir.dt.from_np(_np.dtype(dtype))
        args.append(nc.dram_tensor(f"out_{i}_dram", shape, dt, kind="ExternalOutput").ap())
    build(nc, *args)
    r = _run(nc, [arrays], core_ids=[0])
    got = tuple(r.results[0][f"out_{i}_dram"] for i in range(len(_OUTS)))
    return got[0]
```

```python
from contextlib import ExitStack

import concourse.bass as bass
from concourse import mybir

ALU = mybir.AluOpType
ACT = mybir.ActivationFunctionType
AX_X = mybir.AxisListType.X
F32 = mybir.dt.float32
F32R = mybir.dt.float32r
BF16 = mybir.dt.bfloat16

P = 128
EPS = 1e-5
MASKED = -1e30
LOWEST = -3e38

GH = 4
RA = 256
AHEAD = 5
HALF = 512
NSTEP = 12
STEPS = GH * NSTEP
RING = 12
LAG = 7
LOW_LAG = 3
POOL_LOW_LAG = 1
POOL_LOW = (1, 4, 6, 9)
ACT_HIGH = (0, 5, 8)
ACT_HIGH_LAG = 1
OUT_LAG = 3


def score_chunks():
    out = []
    for half in range(2):
        for kt in range(4 * (half + 1)):
            q0 = max(HALF * half, P * kt)
            out.append((half, kt, q0, HALF * (half + 1) - q0))
    return out


def max_chunks():
    out = []
    for qt in range(8):
        for part in range(1 + qt // 4):
            k0 = HALF * part
            out.append((qt, part, k0, min(HALF, P * (qt + 1) - k0)))
    return out


CHUNKS = score_chunks()
MAXES = max_chunks()
NMAX = len(MAXES) + 1
assert len(CHUNKS) == NSTEP

MAX_AT = {8: [(2, 0), (2, 1)], 9: [(2, 2)], 10: [(2, 3)], 11: [(2, 4)], 0: [(1, 5)], 1: [(1, 6)],
          2: [(1, 7), (1, 8)], 3: [(1, 9)], 4: [(1, 10)], 5: [(1, 11)], 7: [(1, NMAX - 1)]}
NEARLY = 5
JOIN_AT = 6
PLACE_AT = 8
LOAD_X_AT = 2
LN_STATS_AT, LN_AGGR_AT, LN_NORM_AT = (30, 31), 32, (42, 43)
LN_TURN_AT, LN_MODULATE_AT, LN_SPLIT_AT = (1, 2), (2, 3, 4, 5), 7
LN_LOW_AT = (7, 9)
A_HIGH_LAG, A_LOW_LAG, A_STORE_LAG = 1, 2, 4
QK_RING = 4
A_ITEMS = ["v0", "v1"] + [f"qk{m}" for m in range(8)]
A_PARTS = {"v": 3, "q": 2}
A_AT = dict(zip([13, 14, 16, 18, 19, 21] + [22 + (3 * n) // 2 for n in range(16)],
                [(name, part) for name in A_ITEMS for part in range(A_PARTS[name[0]])]))
assert len(A_AT) == sum(A_PARTS[name[0]] for name in A_ITEMS)
A_DONE_AT = {s: name for s, (name, part) in A_AT.items() if part == A_PARTS[name[0]] - 1}
A_NTURN, A_NITEM = 2, len(A_ITEMS)
A_N = A_NTURN + A_NITEM


ATT_AT, ATT_SPLIT_AT, BASE_AT = 0, 1, 4
PROJECT_AT = (5, 6)
RESIDUAL_AT = (6, 7)
STATS_AT, RSTD_AT, NORM_AT, TURN_AT, REST_AT = 8, 9, 10, 11, 11
ROWS_HI_AT, ROWS_LO_AT = 12, 13
FINISH_AT = OUT_LAG - 1

PIECE_AT = {14: 0, 30: 1}
PIECE_LOW_AT = {17: (0, 0), 20: (0, 1), 33: (1, 0), 36: (1, 1)}


def place(c, others, names):
    mine = [k for k in range(NSTEP) if (k in others) == (c in others)]
    return names[c in others], len(mine), mine.index(c) + 1


def low_place(c):
    return place(c, POOL_LOW, ("prob_lo", "prob_lo_pool"))


def high_place(c):
    return place(c, ACT_HIGH, ("prob_hi", "prob_hi_act"))


def flat(i, s):
    j, c = divmod(s, NSTEP)
    return (i - 1, j + GH, c) if j < 0 else (i, j, c)


def wait(eng, sem, value):
    if isinstance(value, int) and value <= 0:
        return
    eng.wait_ge(sem, value)


def build(nc, x, cond, Wqkv, Wproj, bproj, W1, b1, W2, b2, g1, be1, g2, be2, Wada, bada, out):
    B, T, D = x.shape
    H, HD = 16, 32
    F = W1.shape[1]
    KT = D // P
    FT = F // P
    ROWS = B * T
    QK3 = 3 * D
    SCALE = float(HD) ** -0.5
    VW = 2 * HD + 1
    NIT = B * H // GH
    NA = ROWS // RA
    NR = RA // P
    IPB = H // GH
    assert NIT == NA == 32 and KT == 4 and NR == 2 and T == 1024 and IPB == 4

    x_rows = x.rearrange("b t d -> (b t) d")
    out_rows = out.rearrange("b t d -> (b t) d")
    qk_dram = nc.dram_tensor("qk_split", (2, IPB, 2, P, ROWS), F32, kind="Internal").ap()
    v_dram = nc.dram_tensor("v_split", (ROWS, H, VW), F32, kind="Internal").ap()
    o_dram = nc.dram_tensor("attended", (H, VW, ROWS), F32, kind="Internal").ap()
    r_dram = nc.dram_tensor("inverse_sums", (H, ROWS), F32, kind="Internal").ap()
    mod_dram = nc.dram_tensor("modulation", (6, B, D), F32, kind="Internal").ap()

    with ExitStack() as keep:
        sems = {}

        def sem(name):
            if name not in sems:
                sems[name] = keep.enter_context(nc.semaphore(name))
            return sems[name]

        def sb(stack, name, shape, dt=F32):
            return stack.enter_context(nc.sbuf_tensor(name, shape, dt))

        def sb_full_low(stack, name, shape):
            with nc.sbuf_tensor(name + "_full", shape, F32) as full:
                pass
            return full, sb(stack, name + "_l", shape, F32R)

        def psum(stack, name, shape):
            return stack.enter_context(nc.psum_tensor(name, shape, F32))

        ident = sb(keep, "ident", [P, P])
        coef = sb(keep, "coef", [P, 4, B, KT])
        b1c = sb(keep, "b1c", [P, FT])
        gb = sb(keep, "gb", [P, 4, KT])

        power = sb(keep, "power", [P, NR])

        att = ExitStack()
        wqkv_h = sb(att, "wqkv_h", [P, KT, QK3], F32R)
        wqkv, wqkv_l = sb_full_low(att, "wqkv", [P, KT, QK3])
        mod = sb(att, "mod", [B, 6, D])
        csb = sb(att, "csb", [B, 4, D])
        xin = sb(att, "xin", [P, NR, D])
        xn = sb(att, "xn", [P, NR, D])
        xm_h = sb(att, "xm_h", [P, KT, RA], F32R)
        xm, xm_l = sb_full_low(att, "xm", [P, KT, RA])
        ident_b = sb(att, "ident_b", [P, P], BF16)
        mask_q = sb(att, "mask_q", [P, P], BF16)
        mask_k = sb(att, "mask_k", [P, P], BF16)
        sT = sb(att, "sT", [P, KT, B])
        stats = sb(att, "stats", [P, NR, 6])
        aggr = sb(att, "aggr", [P, NR, 2])
        rstd = sb(att, "rstd", [P, NR])
        veps = sb(att, "veps", [P, NR])
        qk_hl = sb(att, "qk_hl", [P, QK_RING, 2, RA], F32R)
        vaug = sb(att, "vaug", [P, NR, H, VW], F32R)
        with nc.sbuf_tensor("wada", [P, 6, KT, D], F32) as wada:
            pass
        qst = sb(att, "qst", [P, GH, T], F32R)
        e_h = sb(att, "e_h", [P, RING, HALF], F32R)
        e_full, e_l = sb_full_low(att, "e", [P, RING, HALF])
        with nc.sbuf_tensor("bada_sb", [B, 6, D], F32) as bada_sb:
            pass
        kst = sb(att, "kst", [P, GH, T], F32R)
        vst = sb(att, "vst", [P, GH, T // P, VW], F32R)
        o_sb = sb(att, "o_sb", [VW, 2, HALF])
        mx = sb(att, "mx", [P, 2, 8])
        mxc = sb(att, "mxc", [P, 8])
        m_row = sb(att, "m_row", [8, 2, P], F32R)
        psS = psum(att, "psS", [P, 2, HALF])
        psT = psum(att, "psT", [P, 2, HALF])
        psO = psum(att, "psO", [P, 2, HALF])
        psA = psum(att, "psA", [P, 2, HALF])
        att.close()

        mlp = ExitStack()
        NP1 = (F + D) * KT // 1024
        wa_h = sb(mlp, "w1p_h", [P, NP1, 1024], F32R)
        wa, wa_l = sb_full_low(mlp, "w1p", [P, NP1, 1024])
        w1_h, w1_l = (t[:, 0:KT * F // 1024].rearrange("p a b -> p (a b)").rearrange("p (k f) -> p k f", k=KT)
                      for t in (wa_h, wa_l))
        wp_h, wp_l = (t[:, KT * F // 1024:NP1].rearrange("p a b -> p (a b)").rearrange("p (k d) -> p k d", k=KT)
                      for t in (wa_h, wa_l))
        w2_h = sb(mlp, "w2_h", [P, FT, D], F32R)
        w2_full, w2_l = sb_full_low(mlp, "w2", [P, FT, D])
        oin = sb(mlp, "oin", [P, 3, KT, RA])
        a_h = sb(mlp, "a_h", [P, 2, KT, RA], F32R)
        a_full, a_l = sb_full_low(mlp, "a", [P, 2, KT, RA])
        xc = sb(mlp, "xc", [P, NR, D])
        x1 = sb(mlp, "x1", [P, 2, NR, D])
        gate1 = sb(mlp, "gate1", [P, D])
        gate2 = sb(mlp, "gate2", [P, 2, D])
        bias1 = sb(mlp, "bias1", [P, 1, D])
        bias2 = sb(mlp, "bias2", [P, 1, D])
        tmp = sb(mlp, "tmp", [P, 2, D])
        h_h = sb(mlp, "h_h", [P, 4, RA], F32R)
        h_full, h_l = sb_full_low(mlp, "h", [P, 4, RA])
        stats2 = sb(mlp, "stats2", [P, NR, 6])
        aggr2 = sb(mlp, "aggr2", [P, NR, 2])
        rstd2 = sb(mlp, "rstd2", [P, NR])
        veps2 = sb(mlp, "veps2", [P, NR])
        psY = psum(mlp, "psY", [P, NR, D])
        psH = psum(mlp, "psH", [P, 4, D])
        psP = psum(mlp, "psP", [P, 2, D])
        mlp.close()

        qk_loaded = [sem(f"qk_loaded{j}") for j in range(GH)]
        v_loaded = [sem(f"v_loaded{j}") for j in range(GH)]
        m_loaded = [sem(f"m_loaded{j}") for j in range(GH)]
        qk_stored = [sem(f"qk_stored{j}") for j in range(QK_RING)]
        v_stored = [sem(f"v_stored{j}") for j in range(2)]
        o_stored = [sem(f"o_stored{j}") for j in range(2)]
        NQKL = 4 * 16

        w1_v = W1.rearrange("(k p) (h f) -> p k h f", p=P, h=2)
        w2_v = W2.rearrange("(k p) d -> p k d", p=P)
        wp_v = Wproj.rearrange("(k p) d -> p k d", p=P)
        wq_v = Wqkv.rearrange("(k p) n -> p k n", p=P)
        wa_v = Wada.rearrange("(k p) n -> p k n", p=P)
        W2_PIECES = FT // 2

        def w2_piece(t, n):
            return t[:, 2 * n:2 * n + 2, :]

        def past(eng, name):
            eng.sem_inc(sem(f"past_{name}"), 1)

        def wait_half(eng, where, i, j, c):
            name, a_head, nth = where(c)
            eng.wait_ge(sem(name), (i * GH + j) * a_head + nth)

        block = keep.enter_context(nc.Block())

        @block.sync
        def _(sp):
            sp.dma_start(csb[:, 0], cond).then_inc(sem("cond_loaded"), 16)
            sp.dma_start(bada_sb[:], bada.rearrange("(n d) -> n d", n=6).partition_broadcast(B))\
              .then_inc(sem("bada_loaded"), 16)
            for n, v in enumerate((g1, be1, g2, be2)):
                sp.dma_start(gb[:, n], v).then_inc(sem("small_loaded"), 16)
            sp.dma_start(b1c[:], b1).then_inc(sem("small_loaded"), 16)

            def load_x(ia):
                wait(sp, sem("xn_ready"), ia)
                past(sp, "sp")
                sp.dma_start(xin[:], x_rows[bass.ds(ia * RA, RA)].rearrange("(r p) d -> p r d", p=P))\
                  .then_inc(sem("x_loaded"), 16)

            load_x(0)
            for n in range(6):
                sp.dma_start(wada[:, n], wa_v[:, :, n * D:(n + 1) * D]).then_inc(sem(f"wada_loaded{n}"), 16)
                if n == 1:
                    for k in range(KT):
                        sp.dma_start(wqkv[:, k], wq_v[:, k]).then_inc(sem(f"wqkv_loaded{k}"), 16)
            def store_modulation(first, end):
                sp.wait_ge(sem("mod_ready"), end)
                past(sp, "sp")
                sp.dma_start(mod_dram[first:end].rearrange("n b d -> b n d"), mod[:, first:end])\
                  .then_inc(sem("mod_stored"), 16)

            def a_store(ia, name):
                idx = A_ITEMS.index(name)
                sp.wait_ge(sem("a_hi_done"), ia * A_N + A_NTURN + idx + 1)
                past(sp, "sp")
                sp.wait_ge(sem("a_lo_done"), ia * A_NITEM + idx + 1)
                past(sp, "sp")
                if name[0] == "v":
                    r = int(name[1:])
                    sp.dma_start(v_dram[bass.ds(ia * RA + r * P, P)].rearrange("p h c -> p (h c)"),
                                  vaug[:, r].rearrange("p h c -> p (h c)").bitcast(F32)).then_inc(v_stored[r], 16)
                else:
                    m = int(name[2:])
                    sp.dma_start(qk_dram[m // IPB, m % IPB, :, :, bass.ds(ia * RA, RA)].rearrange("a p r -> p a r"),
                                  qk_hl[:, m % QK_RING].bitcast(F32)).then_inc(qk_stored[m % QK_RING], 16)

            def o_store(i, j, half):
                sp.wait_ge(sem("o_copied"), (i * GH + j) * 2 + half + 1)
                past(sp, "sp")
                b, hg = i // IPB, i % IPB
                cols = bass.ds(b * T + half * HALF, HALF)
                dst = o_dram[hg * GH + j, :, cols] if isinstance(i, int) else \
                    o_dram[bass.ds(hg * GH + j, 1), :, cols].rearrange("a c r -> (a c) r")
                sp.dma_start(dst, o_sb[:, half, :]).then_inc(o_stored[half], 16)

            def a_stores(ia):
                for name in A_ITEMS:
                    a_store(ia, name)

            store_modulation(0, 2)
            load_x(1)
            a_stores(0)
            store_modulation(2, 6)
            with sp.Fori(1, AHEAD) as ia:
                load_x(ia + 1)
                a_stores(ia)

            def load_qk(i, j):
                b, hg = i // IPB, i % IPB
                done = (b + 1) * IPB
                if j == 0:
                    for s in range(QK_RING):
                        wait(sp, qk_stored[s], done * (8 // QK_RING * 16))
                        past(sp, "sp")
                    for s in range(2):
                        wait(sp, v_stored[s], done * 16)
                        past(sp, "sp")
                wait(sp, sem("scores_ready"), i * (GH * NSTEP) - (GH - 1 - j) * NSTEP
                     if not isinstance(i, int) or i > 0 else 0)
                past(sp, "sp")
                for tile, kind in ((kst, 1), (qst, 0)):
                    src = qk_dram[kind, hg] if isinstance(i, int) else \
                        qk_dram[kind, bass.ds(hg, 1)].rearrange("a s p r -> (a s) p r")
                    src = src[:, HD * j:HD * (j + 1), bass.ds(b * T, T)]
                    pairs = ((0, 2, src), (2, 1, src[0])) if kind == 1 else ((1, 2, src), (0, 1, src[0]))
                    for first, n, what in pairs:
                        sp.dma_start(tile[HD * first:HD * (first + n), j, :].bitcast(F32), what)\
                          .then_inc(qk_loaded[j], 16)

            def load_v(i, j):
                b, hg = i // IPB, i % IPB
                wait(sp, sem("pv_done"), i * (GH * NSTEP) - (GH - 1 - j) * NSTEP
                     if not isinstance(i, int) or i > 0 else 0)
                past(sp, "sp")
                src = v_dram[bass.ds(b * T, T)].rearrange("(k p) h c -> p k h c", p=P)
                if isinstance(i, int):
                    src = src[:, :, hg * GH + j]
                else:
                    src = src[:, :, bass.ds(hg * GH + j, 1)].rearrange("p k h c -> p k (h c)")
                sp.dma_start(vst[:, j].bitcast(F32), src).then_inc(v_loaded[j], 16)

            def place_max(i, j):
                wait(sp, sem("max_done"), (i * GH + j + 1) * NMAX)
                past(sp, "sp")
                sp.dma_start(qst[96:97, j, :].bitcast(F32), m_row[:, j % 2, :].bitcast(F32)).then_inc(m_loaded[j], 16)

            for j in range(GH):
                load_qk(0, j)
                if j == 0:
                    place_max(0, 0)
            for j in range(GH):
                load_v(0, j)

            def load_piece(i):
                n = (i - (NIT - AHEAD)) * 2
                sp.wait_ge(sem("a_formed"), NA * A_N)
                wait(sp, sem("w1p_hi"), n)
                for q in range(2):
                    if isinstance(i, int) and i == NIT - 1:
                        src = wp_v[:, 2 * q:2 * q + 2]
                        dst = wa[:, n + q].rearrange("p (k d) -> p k d", k=2)
                    else:
                        src = w1_v[:, bass.ds(i - (NIT - AHEAD), 1), q].rearrange("p k f -> p (k f)")
                        dst = wa[:, bass.ds(n + q, 1)].rearrange("p a f -> p (a f)")
                    sp.dma_start(dst, src).then_inc(sem(f"w1p_loaded{q}"), 16)

            def o_stores(i, s):
                for half, end in ((0, 4), (1, NSTEP)):
                    at = s - end - LAG - 1
                    if at % NSTEP == 0 and not (isinstance(i, int) and i == 0 and at < 0):
                        ii, j, _ = flat(i, at)
                        o_store(ii, j, half)

            def iteration(i, with_a, before_a, last=False, pieces=False):
                first = isinstance(i, int) and i == 0
                for s in range(STEPS):
                    j, c = divmod(s, NSTEP)
                    nxt = (i, GH - 1) if j == 0 else (i + 1, j - 1)
                    reload = not (first and j == 0) and not (last and j > 0)
                    if c == 0 and reload:
                        load_qk(*nxt)
                    if c == PLACE_AT and not (last and j == GH - 1):
                        place_max(i + (j + 1) // GH, (j + 1) % GH)
                    if c == LAG + 1 and reload:
                        load_v(*nxt)
                    o_stores(i, s)
                    if with_a and s - A_STORE_LAG in A_DONE_AT:
                        a_store(i + AHEAD, A_DONE_AT[s - A_STORE_LAG])
                    if before_a and s - A_STORE_LAG + STEPS in A_DONE_AT:
                        a_store(i + AHEAD - 1, A_DONE_AT[s - A_STORE_LAG + STEPS])
                    if with_a and s == LOAD_X_AT and not (isinstance(i, int) and i == NIT - AHEAD - 1):
                        load_x(i + AHEAD + 1)
                    if pieces and s == 2:
                        load_piece(i)

            iteration(0, True, False)
            with sp.Fori(1, NIT - AHEAD - 1) as i:
                iteration(i, True, True)
            iteration(NIT - AHEAD - 1, True, True)
            iteration(NIT - AHEAD, False, True, pieces=True)
            with sp.Fori(NIT - AHEAD + 1, NIT - 1) as i:
                iteration(i, False, False, pieces=True)
            iteration(NIT - 1, False, False, last=True, pieces=True)
            for s in range(LAG + 2):
                o_stores(NIT, s)

            for s in range(2):
                sp.wait_ge(o_stored[s], 16 * NIT * GH)
            by_rows = "h (s r) -> s h r"

            def sums_view(t):
                return t.rearrange("p r d -> p (r d)").rearrange("p (h r) -> p h r", h=H)

            sp.dma_start(sums_view(x1[:, 0]), o_dram[:, 2 * HD].rearrange(by_rows, s=P)).then_inc(sem("sums_loaded"), 16)

            def load_attended(u, parts=(0, 1, 2)):
                rows = bass.ds(u * RA, RA)
                wait(sp, sem("att_ready"), u)
                o_v = o_dram.rearrange("(k j) c r -> j c k r", j=GH)
                r_v = r_dram.rearrange("(k j) r -> j k r", j=GH)
                for j in range(GH):
                    for part in parts:
                        src = o_v[j, HD * part:HD * (part + 1), :, rows] if part < 2 else \
                            r_v[j, :, rows].partition_broadcast(HD)
                        sp.dma_start(oin[HD * j:HD * (j + 1), part], src).then_inc(sem("o_loaded"), 16)

            def load_gate(dst, m, u, done):
                b = u // IPB
                src = mod_dram[m, b] if isinstance(u, int) else \
                    mod_dram[m, bass.ds(b, 1)].rearrange("a d -> (a d)")
                sp.dma_start(dst, src.partition_broadcast(P)).then_inc(done, 16)

            def load_x_gate(u):
                wait(sp, sem("x1_based"), u)
                load_gate(gate1[:], 2, u, sem("gate1_loaded"))
                for dst, src in ((bias1[:, 0], bproj), (bias2[:, 0], b2)):
                    sp.dma_start(dst, src.partition_broadcast(P)).then_inc(sem("gate1_loaded"), 16)
                wait(sp, sem("turned2"), 2 * u)
                sp.dma_start(xc[:], x_rows[bass.ds(u * RA, RA)].rearrange("(r p) d -> p r d", p=P))\
                  .then_inc(sem("xc_loaded"), 16)

            def load_gate2(u, par):
                wait(sp, sem("y_added"), 2 * (u - 1) if not isinstance(u, int) or u > 0 else 0)
                load_gate(gate2[:, par], 5, u, sem("gate2_loaded"))

            def store_rows(u, par):
                sp.wait_ge(sem("y_added"), 2 * u + 2)
                sp.dma_start(out_rows[bass.ds(u * RA, RA)].rearrange("(r p) d -> p r d", p=P), x1[:, par])\
                  .then_inc(sem(f"out_stored{par}"), 16)

            def during(u, par, stores, loads):
                if stores:
                    store_rows(u - 1, 1 - par)
                load_gate2(u + 1, 1 - par)
                if loads:
                    load_attended(u + 2)
                    load_x_gate(u + 2)

            load_attended(0, (0, 1))
            sp.wait_ge(sem("mod_stored"), 32)
            load_x_gate(0)
            load_gate2(0, 0)
            sp.wait_ge(sem("sums_inverted"), 1)
            sp.dma_start(r_dram.rearrange(by_rows, s=P), sums_view(x1[:, 1]))\
              .then_inc(sem("inverses_stored"), 16)
            sp.wait_ge(sem("inverses_stored"), 16)
            load_attended(0, (2,))
            load_attended(1)
            load_x_gate(1)
            during(0, 0, False, True)
            during(1, 1, True, True)
            with sp.Fori(1, NA // 2 - 1) as uu:
                for par in range(2):
                    during(uu * 2 + par, par, True, True)
            during(NA - 2, 0, True, False)
            store_rows(NA - 2, 0)
            store_rows(NA - 1, 1)
            for par in range(2):
                sp.wait_ge(sem(f"out_stored{par}"), 16 * (NA // 2))

        @block.tensor
        def _(pe):
            pe.wait_ge(sem("ident_ready"), 2)
            pe.wait_ge(sem("silu_ready"), 1)
            for k in range(KT):
                mm = pe.transpose(psA[:, 0, k * B:(k + 1) * B], csb[:, 3, k * P:(k + 1) * P], ident[0:B, 0:B])
            mm.then_inc(sem("cond_turned"), 1)
            pe.wait_ge(sem("cond_copied"), 1)

            def modulation(first, end):
                for n in range(first, end + 1):
                    if n < end:
                        pe.wait_ge(sem(f"wada_loaded{n}"), 16)
                        wait(pe, sem("mod_ready"), n - 1)
                        for k in range(KT):
                            mm = pe.matmul(psT[0:B, n % 2, :], sT[:, k, :], wada[:, n, k, :],
                                           start=(k == 0), stop=(k == KT - 1))
                        mm.then_inc(sem("mod_formed"), 1)
                    if n > first:
                        pe.wait_ge(sem("mod_ready"), n)
                        for k in range(KT):
                            c = ((n - 1) * KT + k) * B
                            mm = pe.transpose(psO[:, int(n > 2), c:c + B], mod[:, n - 1, k * P:(k + 1) * P], ident[0:B, 0:B])
                        mm.then_inc(sem("mod_turned"), 1)

            modulation(0, 2)

            def part_a_turn(ia, turns=range(A_NTURN)):
                pe.wait_ge(sem("xn_ready"), ia + 1)
                for n in turns:
                    wait(pe, sem("a_lo_done"), ia * A_NITEM - 1 + n if not isinstance(ia, int) or ia > 0 else 0)
                    for k in range(2):
                        for r in range(NR):
                            mm = pe.transpose(psA[:, n, k * RA + r * P:k * RA + (r + 1) * P],
                                              xn[:, r, (2 * n + k) * P:(2 * n + k + 1) * P], ident[:])
                    mm.then_inc(sem("a_formed"), 1)

            def part_a(ia, name, part=None):
                idx = A_NTURN + A_ITEMS.index(name)
                parts = A_PARTS[name[0]]
                share = range(3 * KT) if part is None else range(3 * KT * part // parts, 3 * KT * (part + 1) // parts)
                if idx == A_NTURN and share[0] == 0:
                    pe.wait_ge(sem("xm_hi"), ia + 1)
                    pe.wait_ge(sem("xm_lo_pool"), ia + 1)
                    pe.wait_ge(sem("xm_lo"), ia + 1)
                if share[0] == 0 and idx < 2 * A_NTURN:
                    pe.wait_ge(sem("a_hi_done"), ia * A_N + idx - 1)
                if share[0] == 0 and idx >= 2 * A_NTURN:
                    pe.wait_ge(sem("a_lo_done"), ia * A_NITEM + idx - A_NTURN - 1)
                at = int(name[1:]) if name[0] == "v" else int(name[2:])
                for n in share:
                    k = n // 3
                    ends = dict(start=(n == 0), stop=(n == 3 * KT - 1), skip_group_check=True)
                    if name[0] == "v":
                        a, w = ((xm_h, wqkv_h), (xm_h, wqkv_l), (xm_l, wqkv_h))[n % 3]
                        mm = pe.matmul(psA[:, idx % 2, :], a[:, k, at * P:(at + 1) * P], w[:, k, 2 * D:3 * D], **ends)
                    else:
                        a, w = ((xm_h, wqkv_h), (xm_l, wqkv_h), (xm_h, wqkv_l))[n % 3]
                        mm = pe.matmul(psA[:, idx % 2, 0:RA], w[:, k, at * P:(at + 1) * P], a[:, k, :], **ends)
                if share[-1] == 3 * KT - 1:
                    mm.then_inc(sem("a_formed"), 1)

            def max_item(i, j, n, between=None):
                head = i * GH + j
                if n == 0:
                    pe.wait_ge(qk_loaded[j], (i + 1) * NQKL)
                wait(pe, sem("max_done"), head * NMAX + n - 1)
                bank = psS[:, (j + n) % 2, :]
                if n == NMAX - 1:
                    pe.wait_ge(sem("max_joined"), head + 1)
                    pe.transpose(bank[0:8, 0:P], mxc[:], ident[:]).then_inc(sem("max_formed"), 1)
                    return
                qt, part, k0, w = MAXES[n]
                diag = k0 + w == P * (qt + 1)
                mm = pe.matmul(bank[:, 0:w], qst[0:96, j, qt * P:(qt + 1) * P], kst[0:96, j, k0:k0 + w],
                               start=True, stop=True)
                if between:
                    between()
                if diag:
                    mm = pe.matmul(bank[:, w - P:w], ident_b[:], mask_q[:], start=False, stop=True,
                                   skip_group_check=True)
                mm.then_inc(sem("max_formed"), 1)

            def scores(i, j, c, between=None):
                n = i * (GH * NSTEP) + j * NSTEP + c
                if c == 0:
                    pe.wait_ge(m_loaded[j], (i + 1) * 16)
                wait(pe, sem("exp_done"), n - 1)
                _, kt, q0, w = CHUNKS[c]
                bank = psT[:, c % 2, :]
                diag = q0 == P * kt
                mm = pe.matmul(bank[:, 0:w], kst[0:97, j, kt * P:(kt + 1) * P], qst[0:97, j, q0:q0 + w],
                               start=True, stop=True)
                if not diag:
                    mm.then_inc(sem("scores_ready"), 1)

                def mask():
                    pe.matmul(bank[:, 0:P], ident_b[:], mask_k[:], start=False, stop=True,
                              skip_group_check=True).then_inc(sem("scores_ready"), 1)

                if between:
                    between(mask if diag else None)
                elif diag:
                    mask()

            def values(i, j, c):
                n = i * (GH * NSTEP) + j * NSTEP + c
                slot = (j * NSTEP + c) % RING
                half, kt, q0, w = CHUNKS[c]
                if c == 0:
                    pe.wait_ge(v_loaded[j], (i + 1) * 16)
                if kt == 0:
                    wait(pe, sem("o_copied"), (i * GH + j) * 2 + half - 1)
                wait_half(pe, low_place, i, j, c)
                o = psO[0:VW, half, q0 - HALF * half:q0 - HALF * half + w]
                pe.matmul(o, vst[:, j, kt, :], e_h[:, slot, 0:w], start=(kt == 0), stop=True,
                          skip_group_check=True)
                pe.matmul(o, vst[:, j, kt, :], e_l[:, slot, 0:w], start=False, stop=True,
                          skip_group_check=True).then_inc(sem("pv_done"), 1)

            def iteration(i, with_a, last):
                for s in range(STEPS):
                    j, c = divmod(s, NSTEP)
                    items = [(i + (j + d) // GH, (j + d) % GH, n) for d, n in MAX_AT.get(c, ())
                             if not (last and j + d >= GH)]
                    if items and items[0][2] < NMAX - 1:
                        scores(i, j, c, lambda mask: max_item(*items[0], between=mask))
                        items = items[1:]
                    else:
                        scores(i, j, c)
                    for item in items:
                        max_item(*item)
                    if with_a and s in LN_TURN_AT:
                        part_a_turn(i + AHEAD, (LN_TURN_AT.index(s),))
                    if with_a and s in A_AT:
                        part_a(i + AHEAD, *A_AT[s])
                    if not (isinstance(i, int) and i == 0 and s < LAG):
                        values(*flat(i, s - LAG))

            pe.wait_ge(sem("wqkv_lo"), KT)
            part_a_turn(0)
            for name in A_ITEMS:
                part_a(0, name)
            modulation(2, 6)
            part_a_turn(1)
            with pe.Fori(1, AHEAD - 1) as ia:
                for name in A_ITEMS:
                    part_a(ia, name)
                part_a_turn(ia + 1)
            for name in A_ITEMS:
                part_a(AHEAD - 1, name)
            pe.wait_ge(sem("kst_set"), 1)
            pe.wait_ge(sem("masks_ready"), 2)
            for head, items in ((0, NMAX), (1, NEARLY)):
                for n in range(items):
                    max_item(0, head, n)
            iteration(0, True, False)
            with pe.Fori(1, NIT - AHEAD) as i:
                iteration(i, True, False)
            with pe.Fori(NIT - AHEAD, NIT - 1) as i:
                iteration(i, False, False)
            iteration(NIT - 1, False, True)
            for s in range(LAG):
                values(*flat(NIT, s - LAG))

            def project(u, par, r):
                pe.wait_ge(sem("att_lo"), u + 1)
                wait(pe, sem("y2_done"), 2 * (u - 1) + r + 1 if not isinstance(u, int) or u > 0 else 0)
                n = 0
                for k in range(KT):
                    for a, w in ((a_h, wp_h), (a_h, wp_l), (a_l, wp_h)):
                        mm = pe.matmul(psP[:, r, :], a[:, par, k, r * P:(r + 1) * P], w[:, k, :],
                                       start=(n == 0), stop=(n == 3 * KT - 1))
                        n += 1
                mm.then_inc(sem("projected"), 1)

            def turn2(u):
                pe.wait_ge(sem("xn2_ready"), u + 1)
                for n in range(2):
                    for k in range(2):
                        for r in range(NR):
                            mm = pe.transpose(psP[:, n, k * RA + r * P:k * RA + (r + 1) * P],
                                              xc[:, r, (2 * n + k) * P:(2 * n + k + 1) * P], ident[:])
                    mm.then_inc(sem("turned2"), 1)

            def hidden(u, par, m):
                if m == 0:
                    pe.wait_ge(sem("rows_lo"), u + 1)
                wait(pe, sem("gelu_done"), u * FT + m - 3)
                n = 0
                for k in range(KT):
                    for w, a in ((w1_h, a_h), (w1_h, a_l), (w1_l, a_h)):
                        mm = pe.matmul(psH[:, m % 4, 0:RA], w[:, k, m * P:(m + 1) * P], a[:, par, k, :],
                                       start=(n == 0), stop=(n == 3 * KT - 1))
                        n += 1
                mm.then_inc(sem("hidden_ready"), 1)

            def mlp_out(u, m):
                if isinstance(u, int) and u == 0 and m % 2 == 0:
                    pe.wait_ge(sem("w2_lo"), m // 2 + 1)
                pe.wait_ge(sem("h_lo"), u * FT + m + 1)
                for r in range(NR):
                    if m == 0:
                        wait(pe, sem("gated2"), 2 * u - 1 + r if not isinstance(u, int) or u > 0 else 0)
                    for n, (a, w) in enumerate(((h_h, w2_h), (h_h, w2_l), (h_l, w2_h))):
                        mm = pe.matmul(psY[:, r, :], a[:, m % 4, r * P:(r + 1) * P], w[:, m, :],
                                       start=(m == 0 and n == 0), stop=(m == FT - 1 and n == 2),
                                       skip_group_check=True)
                mm.then_inc(sem("mlp_done"), 1)

            def rows(u, par, prepare):
                for m in range(FT):
                    hidden(u, par, m)
                    if prepare:
                        if m in PROJECT_AT:
                            project(u + 1, 1 - par, PROJECT_AT.index(m))
                        if m == TURN_AT:
                            turn2(u + 1)
                    if m >= OUT_LAG:
                        mlp_out(u, m - OUT_LAG)
                    elif not (isinstance(u, int) and u == 0):
                        mlp_out(u - 1, FT + m - OUT_LAG)

            pe.wait_ge(sem("w1p_lo"), 2 * NP1)
            for r in range(NR):
                project(0, 0, r)
            turn2(0)
            for par in range(2):
                rows(par, par, True)
            with pe.Fori(1, NA // 2 - 1) as uu:
                for par in range(2):
                    rows(uu * 2 + par, par, True)
            rows(NA - 2, 0, True)
            rows(NA - 1, 1, False)
            for m in range(FT - OUT_LAG, FT):
                mlp_out(NA - 1, m)

        @block.scalar
        def _(act):
            act.wait_ge(sem("cond_loaded"), 16)
            act.activation(csb[:, 1], csb[:, 0], ACT.Exp, scale=-1.0).then_inc(sem("cond_exp"), 1)
            act.wait_ge(sem("cond_turned"), 1)
            act.activation(sT[:].rearrange("p k b -> p (k b)"), psA[:, 0, 0:KT * B], ACT.Copy)\
               .then_inc(sem("cond_copied"), 1)

            def a_modulate(ia, tiles=range(KT)):
                b = ia // IPB
                for kk in tiles:
                    n, k = divmod(kk, 2)
                    if k == 0:
                        act.wait_ge(sem("a_formed"), ia * A_N + n + 1)
                    ca, cb = (coef[:, w, b, kk:kk + 1] if isinstance(ia, int) else
                              coef[:, w, bass.ds(b, 1), kk] for w in (0, 1))
                    a = act.activation(xm[:, kk, :], psA[:, n, k * RA:(k + 1) * RA], ACT.Identity,
                                       scale=ca, bias=cb)
                    if k == 1:
                        a.then_inc(sem("a_hi_done"), 1)

            def a_high(ia, name):
                idx = A_NTURN + A_ITEMS.index(name)
                if name[0] == "v":
                    r = int(name[1:])
                    wait(act, v_stored[r], ia * 16)
                    dst = vaug[:, r, :, 0:HD]
                    src = psA[:, idx % 2, :].rearrange("p (h c) -> p h c", c=HD)
                else:
                    m = int(name[2:])
                    wait(act, qk_stored[m % QK_RING], (ia * (8 // QK_RING) + m // QK_RING) * 16)
                    dst, src = qk_hl[:, m % QK_RING, 0], psA[:, idx % 2, 0:RA]
                act.wait_ge(sem("a_formed"), ia * A_N + idx + 1)
                act.activation(dst, src, ACT.Copy).then_inc(sem("a_hi_done"), 1)

            def exps(i, j, c):
                n = i * (GH * NSTEP) + j * NSTEP + c
                slot = (j * NSTEP + c) % RING
                w = CHUNKS[c][3]
                wait(act, sem("pv_done"), n - RING + 1)
                act.wait_ge(sem("scores_ready"), n + 1)
                act.activation(e_full[:, slot, 0:w], psT[:, c % 2, 0:w], ACT.Exp, scale=SCALE)\
                   .then_inc(sem("exp_done"), 1)

            def prob_high(i, s):
                if isinstance(i, int) and i == 0 and s < ACT_HIGH_LAG:
                    return
                i, j, c = flat(i, s - ACT_HIGH_LAG)
                if c in ACT_HIGH:
                    slot = (j * NSTEP + c) % RING
                    w = CHUNKS[c][3]
                    act.wait_ge(sem("exp_done"), i * (GH * NSTEP) + j * NSTEP + c + 1)
                    act.activation(e_h[:, slot, 0:w], e_full[:, slot, 0:w], ACT.Copy).then_inc(sem("prob_hi_act"), 1)

            def o_copy(i, j, half):
                head = i * GH + j
                wait(act, o_stored[half], head * 16)
                act.wait_ge(sem("pv_done"), head * NSTEP + (4 if half == 0 else NSTEP))
                act.activation(o_sb[:, half, :], psO[0:VW, half, :], ACT.Copy).then_inc(sem("o_copied"), 1)

            def outputs(i, s):
                for half, end in ((0, 4), (1, NSTEP)):
                    at = s - end - LAG
                    if at % NSTEP == 0 and not (isinstance(i, int) and i == 0 and at < 0):
                        ii, j, _ = flat(i, at)
                        o_copy(ii, j, half)

            def piece_high(i, q):
                n = (i - (NIT - AHEAD)) * 2 + q
                act.wait_ge(sem(f"w1p_loaded{q}"), (i - (NIT - AHEAD) + 1) * 16)
                act.activation(wa_h[:, bass.ds(n, 1)], wa[:, bass.ds(n, 1)], ACT.Copy)\
                   .then_inc(sem("w1p_hi"), 1)

            def iteration(i, with_a):
                for s in range(STEPS):
                    exps(i, *divmod(s, NSTEP))
                    prob_high(i, s)
                    outputs(i, s)
                    if with_a and s in LN_MODULATE_AT:
                        a_modulate(i + AHEAD, (LN_MODULATE_AT.index(s),))
                    if with_a and s - A_HIGH_LAG in A_DONE_AT:
                        a_high(i + AHEAD, A_DONE_AT[s - A_HIGH_LAG])
                    if not with_a and s in PIECE_AT:
                        piece_high(i, PIECE_AT[s])

            def a_products(ia):
                for name in A_ITEMS:
                    a_high(ia, name)

            for k in range(KT):
                act.wait_ge(sem(f"wqkv_loaded{k}"), 16)
                act.activation(wqkv_h[:, k, :], wqkv[:, k, :], ACT.Copy).then_inc(sem("wqkv_hi"), 1)
            act.wait_ge(sem("coef_ready"), 1)
            a_modulate(0)
            a_products(0)
            a_modulate(1)
            with act.Fori(1, AHEAD - 1) as ia:
                a_products(ia)
                a_modulate(ia + 1)
            a_products(AHEAD - 1)
            iteration(0, True)
            with act.Fori(1, NIT - AHEAD) as i:
                iteration(i, True)
            with act.Fori(NIT - AHEAD, NIT) as i:
                iteration(i, False)
            for s in range(LAG + 1):
                if s < ACT_HIGH_LAG:
                    prob_high(NIT, s)
                outputs(NIT, s)

            for half in range(2):
                act.wait_ge(o_stored[half], 16 * NIT * GH)
            for n in range(W2_PIECES):
                if n == 0:
                    act.wait_ge(sem("sums_loaded"), 16)
                if n == 2:
                    act.wait_ge(sem("o_loaded"), 12 * 16)
                act.dma_start(w2_piece(w2_full, n), w2_piece(w2_v, n)).then_inc(sem(f"w2_loaded{n}"), 16)

            def modulate2(u, par):
                b = u // IPB
                for n in range(2):
                    act.wait_ge(sem("turned2"), 2 * u + n + 1)
                    for k in range(2):
                        kk = 2 * n + k
                        ca, cb = (coef[:, w, b, kk:kk + 1] if isinstance(u, int) else
                                  coef[:, w, bass.ds(b, 1), kk] for w in (2, 3))
                        a = act.activation(a_full[:, par, kk, :], psP[:, n, k * RA:(k + 1) * RA],
                                           ACT.Identity, scale=ca, bias=cb)
                    a.then_inc(sem("y2_done"), 1)

            def gelu(u, m):
                wait(act, sem("mlp_done"), u * FT + m - 3)
                act.wait_ge(sem("hidden_ready"), u * FT + m + 1)
                act.activation(h_full[:, m % 4, :], psH[:, m % 4, 0:RA], ACT.Gelu, bias=b1c[:, m:m + 1])\
                   .then_inc(sem("gelu_done"), 1)

            def rows(u, par, prepare):
                for m in range(FT):
                    gelu(u, m)
                    if prepare and m == TURN_AT:
                        modulate2(u + 1, 1 - par)

            act.wait_ge(sem("small_loaded"), 5 * 16)
            modulate2(0, 0)
            for par in range(2):
                rows(par, par, True)
            with act.Fori(1, NA // 2 - 1) as uu:
                for par in range(2):
                    rows(uu * 2 + par, par, True)
            rows(NA - 2, 0, True)
            rows(NA - 1, 1, False)

        @block.vector
        def _(dve):
            dve.memset(mx[:], LOWEST).then_inc(sem("mx_set"), 1)
            dve.memset(kst[96:97].bitcast(F32), -1.0).then_inc(sem("kst_set"), 1)
            dve.wait_ge(sem("cond_exp"), 1)
            dve.tensor_scalar_add(csb[:, 1], csb[:, 1], 1.0).then_inc(sem("silu_step"), 1)
            dve.wait_ge(sem("silu_step"), 1)
            dve.reciprocal(csb[:, 2], csb[:, 1]).then_inc(sem("silu_step"), 1)
            dve.wait_ge(sem("silu_step"), 2)
            dve.tensor_tensor(csb[:, 3], csb[:, 0], csb[:, 2], ALU.mult).then_inc(sem("silu_ready"), 1)

            def wqkv_low(k):
                dve.wait_ge(sem("wqkv_hi"), k + 1)
                dve.tensor_tensor(wqkv_l[:, k, :], wqkv[:, k, :], wqkv_h[:, k, :].bitcast(F32),
                                  ALU.subtract).then_inc(sem("wqkv_lo"), 1)

            dve.wait_ge(sem("bada_loaded"), 16)

            def modulation(first, end):
                for n in range(first, end):
                    dve.wait_ge(sem("mod_formed"), n + 1)
                    dve.tensor_tensor(mod[:, n], psT[0:B, n % 2, :], bada_sb[:, n], ALU.add)\
                       .then_inc(sem("mod_ready"), 1)

            def coefficients(c, shift, scale):
                dve.wait_ge(sem("mod_turned"), 2 + 4 * c)
                turned = psO[:, c, 0:6 * KT * B].rearrange("p (n k b) -> p n k b", n=6, k=KT)
                for k in range(KT):
                    for w in range(2):
                        dve.tensor_scalar(coef[:, 2 * c + w, :, k], turned[:, scale, k, :], 1.0,
                                          gb[:, 2 * c + w, k:k + 1], ALU.add, ALU.mult).then_inc(sem("coef_step"), 1)
                dve.wait_ge(sem("coef_step"), 2 * KT * (c + 1))
                dve.tensor_tensor(coef[:, 2 * c + 1].rearrange("p b k -> p k b"),
                                  coef[:, 2 * c + 1].rearrange("p b k -> p k b"), turned[:, shift], ALU.add)\
                   .then_inc(sem("coef_ready"), 1)

            modulation(0, 2)
            dve.wait_ge(sem("small_loaded"), 5 * 16)
            coefficients(0, 0, 1)
            for k in range(KT):
                wqkv_low(k)

            def ln_stats(ia, r):
                dve.wait_ge(sem("x_loaded"), 16 * (ia + 1))
                dve.bn_stats(stats[:, r], xin[:, r]).then_inc(sem("ln_stats"), 1)

            def ln_aggregate(ia):
                for r in range(NR):
                    dve.wait_ge(sem("ln_stats"), ia * NR + r + 1)
                    past(dve, "dve")
                    dve.bn_aggr(aggr[:, r], stats[:, r]).then_inc(sem("ln_aggr"), 1)
                dve.wait_ge(sem("ln_aggr"), ia * NR + NR)
                dve.tensor_scalar_add(veps[:], aggr[:, :, 1], EPS).then_inc(sem("ln_veps"), 1)

            def normalise(ia, r):
                dve.wait_ge(sem("ln_rstd"), ia + 1)
                wait(dve, sem("a_formed"), ia * A_N - A_NITEM if not isinstance(ia, int) or ia > 0 else 0)
                a = dve.tensor_scalar(xn[:, r], xin[:, r], aggr[:, r, 0:1], rstd[:, r:r + 1],
                                      ALU.subtract, ALU.mult)
                if r == NR - 1:
                    a.then_inc(sem("xn_ready"), 1)

            def layer_norm(ia):
                for r in range(NR):
                    ln_stats(ia, r)
                ln_aggregate(ia)
                for r in range(NR):
                    normalise(ia, r)

            def a_split(ia):
                dve.wait_ge(sem("a_hi_done"), ia * A_N + A_NTURN)
                wait(dve, sem("a_formed"), ia * A_N)
                dve.tensor_copy(xm_h[:], xm[:]).then_inc(sem("xm_hi"), 1)

            def a_split_low(ia):
                k = slice(KT // 2, KT)
                dve.wait_ge(sem("xm_hi"), ia + 1)
                dve.tensor_tensor(xm_l[:, k], xm[:, k], xm_h[:, k].bitcast(F32), ALU.subtract)\
                   .then_inc(sem("xm_lo"), 1)

            def a_low(ia, name):
                idx = A_NTURN + A_ITEMS.index(name)
                dve.wait_ge(sem("a_hi_done"), ia * A_N + idx + 1)
                if name[0] == "v":
                    r = int(name[1:])
                    src = psA[:, idx % 2, :].rearrange("p (h c) -> p h c", c=HD)
                    hi, lo = vaug[:, r, :, 0:HD], vaug[:, r, :, HD:2 * HD]
                else:
                    m = int(name[2:])
                    src, hi, lo = psA[:, idx % 2, 0:RA], qk_hl[:, m % QK_RING, 0], qk_hl[:, m % QK_RING, 1]
                dve.tensor_tensor(lo, src, hi.bitcast(F32), ALU.subtract).then_inc(sem("a_lo_done"), 1)

            def max_item(i, j, n):
                head = i * GH + j
                if n == NMAX - 1:
                    slot = (j - 2) % GH
                    wait(dve, m_loaded[slot], (i + (j - 2) // GH + 1) * 16)
                    dve.wait_ge(sem("max_formed"), head * NMAX + n + 1)
                    dve.tensor_copy(m_row[:, j % 2, :], psS[0:8, (j + n) % 2, 0:P]).then_inc(sem("max_done"), 1)
                    return
                qt, part, _, w = MAXES[n]
                if n == 0:
                    wait(dve, sem("max_joined"), head)
                dve.wait_ge(sem("max_formed"), head * NMAX + n + 1)
                dve.tensor_reduce(mx[:, part, qt:qt + 1], psS[:, (j + n) % 2, 0:w], AX_X, ALU.max)\
                   .then_inc(sem("max_done"), 1)

            def max_join(i, j):
                head = i * GH + j
                dve.wait_ge(sem("max_done"), head * NMAX + NMAX - 1)
                wait(dve, sem("max_done"), head * NMAX)
                dve.tensor_tensor(mxc[:], mx[:, 0], mx[:, 1], ALU.max).then_inc(sem("max_joined"), 1)

            def prob_low(i, j, c):
                n = i * (GH * NSTEP) + j * NSTEP + c
                slot = (j * NSTEP + c) % RING
                w = CHUNKS[c][3]
                wait_half(dve, high_place, i, j, c)
                dve.tensor_tensor(e_l[:, slot, 0:w], e_full[:, slot, 0:w], e_h[:, slot, 0:w].bitcast(F32),
                                  ALU.subtract).then_inc(sem("prob_lo"), 1)

            def low_step(i, s):
                if isinstance(i, int) and i == 0 and s < LOW_LAG:
                    return
                at = flat(i, s - LOW_LAG)
                if at[2] not in POOL_LOW:
                    prob_low(*at)

            def iteration(i, with_a, with_ln, last=False):
                for s in range(STEPS):
                    j, c = divmod(s, NSTEP)
                    for d, n in MAX_AT.get(c, ()):
                        if not (last and j + d >= GH):
                            max_item(i + (j + d) // GH, (j + d) % GH, n)
                    if c == JOIN_AT and not (last and j + 1 >= GH):
                        max_join(i + (j + 1) // GH, (j + 1) % GH)
                    if with_ln and s in LN_STATS_AT:
                        ln_stats(i + AHEAD + 1, LN_STATS_AT.index(s))
                    if with_ln and s == LN_AGGR_AT:
                        ln_aggregate(i + AHEAD + 1)
                    if with_ln and s in LN_NORM_AT:
                        normalise(i + AHEAD + 1, LN_NORM_AT.index(s))
                    if with_a and s == LN_SPLIT_AT:
                        a_split(i + AHEAD)
                    if with_a and s == LN_LOW_AT[1]:
                        a_split_low(i + AHEAD)
                    low_step(i, s)
                    if with_a and s - A_LOW_LAG in A_DONE_AT:
                        a_low(i + AHEAD, A_DONE_AT[s - A_LOW_LAG])

            layer_norm(0)
            a_split(0)
            a_split_low(0)
            dve.wait_ge(sem("ones_set"), 2)
            for name in A_ITEMS:
                if name == A_ITEMS[3]:
                    layer_norm(1)
                a_low(0, name)
            modulation(2, 6)
            coefficients(1, 3, 4)
            a_split(1)
            a_split_low(1)
            with dve.Fori(1, AHEAD - 1) as ia:
                for name in A_ITEMS:
                    if name == A_ITEMS[3]:
                        layer_norm(ia + 1)
                    a_low(ia, name)
                a_split(ia + 1)
                a_split_low(ia + 1)
            for name in A_ITEMS:
                if name == A_ITEMS[3]:
                    layer_norm(AHEAD)
                a_low(AHEAD - 1, name)
            dve.wait_ge(sem("mx_set"), 1)
            for head, items in ((0, NMAX), (1, NEARLY)):
                for n in range(items):
                    if n == NMAX - 1:
                        max_join(0, head)
                    max_item(0, head, n)
            iteration(0, True, True)
            with dve.Fori(1, NIT - AHEAD - 1) as i:
                iteration(i, True, True)
            iteration(NIT - AHEAD - 1, True, False)
            with dve.Fori(NIT - AHEAD, NIT - 1) as i:
                iteration(i, False, False)
            iteration(NIT - 1, False, False, last=True)
            for s in range(LOW_LAG):
                low_step(NIT, s)

            dve.wait_ge(sem("sums_loaded"), 16)
            dve.reciprocal(x1[:, 1], x1[:, 0]).then_inc(sem("sums_inverted"), 1)

            def attended(u, par):
                dve.wait_ge(sem("o_loaded"), 12 * 16 * (u + 1))
                dve.tensor_tensor(oin[:, 0], oin[:, 0], oin[:, 1], ALU.add).then_inc(sem("att_joined"), 1)
                dve.wait_ge(sem("att_joined"), u + 1)
                wait(dve, sem("hidden_ready"), (u - 1) * FT if not isinstance(u, int) or u > 1 else 0)
                dve.tensor_tensor(a_full[:, par], oin[:, 0], oin[:, 2], ALU.mult)\
                   .then_inc(sem("att_ready"), 1)

            def attended_split(u, par):
                dve.wait_ge(sem("att_ready"), u + 1)
                dve.tensor_copy(a_h[:, par], a_full[:, par]).then_inc(sem("att_hi"), 1)
                dve.wait_ge(sem("att_hi"), u + 1)
                dve.tensor_tensor(a_l[:, par], a_full[:, par], a_h[:, par].bitcast(F32), ALU.subtract)\
                   .then_inc(sem("att_lo"), 1)

            def base(u):
                dve.wait_ge(sem("gate1_loaded"), 48 * (u + 1))
                dve.tensor_tensor(bias1[:, 0], bias1[:, 0], gate1[:], ALU.mult).then_inc(sem("bias1_ready"), 1)
                dve.wait_ge(sem("bias1_ready"), u + 1)
                dve.wait_ge(sem("xc_loaded"), 16 * (u + 1))
                dve.tensor_tensor(xc[:], xc[:], bias1[:].to_broadcast([P, NR, D]), ALU.add)\
                   .then_inc(sem("xc_based"), 1)

            def residual(u, par, r):
                dve.wait_ge(sem("projected"), u * NR + r + 1)
                wait(dve, sem("y_added"), 2 * (u - 1) + r - 1)
                dve.tensor_tensor(tmp[:, r], psP[:, r], gate1[:], ALU.mult).then_inc(sem("gated"), 1)
                dve.wait_ge(sem("gated"), u * NR + r + 1)
                if r == 0:
                    dve.wait_ge(sem("xc_based"), u + 1)
                    wait(dve, sem(f"out_stored{par}"), (u // 2) * 16 if isinstance(u, int) else u * 8 - 8 * par)
                dve.tensor_tensor(x1[:, par, r], xc[:, r], tmp[:, r], ALU.add).then_inc(sem("x1_step"), 1)

            def statistics(u, par):
                for r in range(NR):
                    dve.wait_ge(sem("x1_step"), u * NR + r + 1)
                    dve.bn_stats(stats2[:, r], x1[:, par, r]).then_inc(sem("ln2_stats"), 1)

            def deviation(u):
                for r in range(NR):
                    dve.wait_ge(sem("ln2_stats"), u * NR + r + 1)
                    past(dve, "dve")
                    dve.bn_aggr(aggr2[:, r], stats2[:, r]).then_inc(sem("ln2_aggr"), 1)
                dve.wait_ge(sem("ln2_aggr"), u * NR + NR)
                dve.tensor_scalar_add(veps2[:], aggr2[:, :, 1], EPS).then_inc(sem("ln2_veps"), 1)

            def norm(u, par):
                dve.wait_ge(sem("ln2_rstd"), u + 1)
                for r in range(NR):
                    a = dve.tensor_scalar(xc[:, r], x1[:, par, r], aggr2[:, r, 0:1], rstd2[:, r:r + 1],
                                          ALU.subtract, ALU.mult)
                a.then_inc(sem("xn2_ready"), 1)

            def rest(u, par):
                dve.wait_ge(sem("gate2_loaded"), 16 * (u + 1))
                dve.tensor_tensor(bias2[:, 0], bias2[:, 0], gate2[:, par], ALU.mult).then_inc(sem("bias2_ready"), 1)
                dve.wait_ge(sem("bias2_ready"), u + 1)
                dve.wait_ge(sem("xn2_ready"), u + 1)
                dve.tensor_tensor(x1[:, par], x1[:, par], bias2[:].to_broadcast([P, NR, D]), ALU.add)\
                   .then_inc(sem("x1_based"), 1)

            def rows_high(u, par):
                dve.wait_ge(sem("y2_done"), 2 * u + 2)
                dve.tensor_copy(a_h[:, par], a_full[:, par]).then_inc(sem("rows_hi"), 1)

            def rows_low(u, par):
                dve.wait_ge(sem("rows_hi"), u + 1)
                dve.tensor_tensor(a_l[:, par], a_full[:, par], a_h[:, par].bitcast(F32), ALU.subtract)\
                   .then_inc(sem("rows_lo"), 1)

            def hidden_high(u, m):
                dve.wait_ge(sem("gelu_done"), u * FT + m + 1)
                dve.tensor_copy(h_h[:, m % 4, :], h_full[:, m % 4, :]).then_inc(sem("h_hi"), 1)

            def finish(u, par):
                dve.wait_ge(sem("mlp_done"), (u + 1) * FT)
                for r in range(NR):
                    wait(dve, sem("x1_step"), u * NR + r + 1)
                    dve.tensor_tensor(tmp[:, r], psY[:, r], gate2[:, par], ALU.mult).then_inc(sem("gated2"), 1)
                for r in range(NR):
                    dve.wait_ge(sem("gated2"), u * NR + r + 1)
                    if r == 0:
                        dve.wait_ge(sem("x1_based"), u + 1)
                    dve.tensor_tensor(x1[:, par, r], x1[:, par, r], tmp[:, r], ALU.add).then_inc(sem("y_added"), 1)

            def prepare_step(u, par, m):
                if m == ATT_AT:
                    attended(u, par)
                if m == ATT_SPLIT_AT:
                    attended_split(u, par)
                if m == BASE_AT:
                    base(u)
                if m in RESIDUAL_AT:
                    residual(u, par, RESIDUAL_AT.index(m))
                if m == STATS_AT:
                    statistics(u, par)
                if m == RSTD_AT:
                    deviation(u)
                if m == NORM_AT:
                    norm(u, par)
                if m == REST_AT:
                    rest(u, par)
                if m == ROWS_HI_AT:
                    rows_high(u, par)
                if m == ROWS_LO_AT:
                    rows_low(u, par)

            def rows(u, par, prepare):
                for m in range(FT):
                    hidden_high(u, m)
                    if m == FINISH_AT and not (isinstance(u, int) and u == 0):
                        finish(u - 1, 1 - par)
                    if prepare:
                        prepare_step(u + 1, 1 - par, m)

            for m in range(FT):
                prepare_step(0, 0, m)
            for par in range(2):
                rows(par, par, True)
            with dve.Fori(1, NA // 2 - 1) as uu:
                for par in range(2):
                    rows(uu * 2 + par, par, True)
            rows(NA - 2, 0, True)
            rows(NA - 1, 1, False)
            finish(NA - 1, 1)

        @block.gpsimd
        def _(pool):
            pool.memset(ident[:], 0.0).then_inc(sem("pool_set"), 1)
            pool.memset(ident_b[:], 0.0).then_inc(sem("pool_set"), 1)
            pool.memset(mask_q[:], 0.0).then_inc(sem("pool_set"), 1)
            pool.memset(mask_k[:], 0.0).then_inc(sem("pool_set"), 1)
            pool.memset(power[:], -0.5).then_inc(sem("pool_set"), 1)
            pool.wait_ge(sem("pool_set"), 5)
            pool.affine_select(out=ident[:], in_=ident[:], compare_op=ALU.not_equal, fill=1.0, base=0,
                               pattern=[[-1, P]], channel_multiplier=1).then_inc(sem("ident_ready"), 1)
            pool.affine_select(out=ident_b[:], in_=ident_b[:], compare_op=ALU.not_equal, fill=1.0, base=0,
                               pattern=[[-1, P]], channel_multiplier=1).then_inc(sem("ident_ready"), 1)
            for r in range(NR):
                pool.memset(vaug[:, r, :, 2 * HD:VW].bitcast(F32), 1.0).then_inc(sem("ones_set"), 1)
            pool.affine_select(out=mask_q[:], in_=mask_q[:], compare_op=ALU.is_ge, fill=MASKED, base=0,
                               pattern=[[-1, P]], channel_multiplier=1).then_inc(sem("masks_ready"), 1)
            pool.affine_select(out=mask_k[:], in_=mask_k[:], compare_op=ALU.is_ge, fill=MASKED, base=0,
                               pattern=[[1, P]], channel_multiplier=-1).then_inc(sem("masks_ready"), 1)

            def low(dst, full, high):
                return pool.tensor_tensor(dst, full, high.bitcast(F32), ALU.subtract)

            def a_rstd(ia):
                pool.wait_ge(sem("ln_veps"), ia + 1)
                pool.tensor_tensor(rstd[:], veps[:], power[:], ALU.pow).then_inc(sem("ln_rstd"), 1)

            def a_split(ia):
                pool.wait_ge(sem("xm_hi"), ia + 1)
                low(xm_l[:, 0:KT // 2], xm[:, 0:KT // 2], xm_h[:, 0:KT // 2]).then_inc(sem("xm_lo_pool"), 1)

            def prob_high(i, j, c):
                n = i * (GH * NSTEP) + j * NSTEP + c
                slot = (j * NSTEP + c) % RING
                w = CHUNKS[c][3]
                pool.wait_ge(sem("exp_done"), n + 1)
                past(pool, "pool")
                pool.tensor_scalar(e_h[:, slot, 0:w], e_full[:, slot, 0:w], 1.0, 1.0, ALU.mult, ALU.mult)\
                    .then_inc(sem("prob_hi"), 1)

            def low_step(i, s):
                if isinstance(i, int) and i == 0 and s < POOL_LOW_LAG:
                    return
                i, j, c = flat(i, s - POOL_LOW_LAG)
                if c in POOL_LOW:
                    slot = (j * NSTEP + c) % RING
                    w = CHUNKS[c][3]
                    wait_half(pool, high_place, i, j, c)
                    low(e_l[:, slot, 0:w], e_full[:, slot, 0:w], e_h[:, slot, 0:w]).then_inc(sem("prob_lo_pool"), 1)

            def piece_low(i, q, part):
                n = (i - (NIT - AHEAD)) * 2 + q
                cols = slice(part * 512, (part + 1) * 512)
                pool.wait_ge(sem("w1p_hi"), n + 1)
                low(wa_l[:, bass.ds(n, 1), cols], wa[:, bass.ds(n, 1), cols], wa_h[:, bass.ds(n, 1), cols]).then_inc(sem("w1p_lo"), 1)

            def iteration(i, with_a, with_ln):
                for s in range(STEPS):
                    if s % NSTEP not in ACT_HIGH:
                        prob_high(i, *divmod(s, NSTEP))
                    low_step(i, s)
                    if with_ln and s == LN_AGGR_AT:
                        a_rstd(i + AHEAD + 1)
                    if with_a and s == LN_LOW_AT[0]:
                        a_split(i + AHEAD)
                    if not with_a and s in PIECE_LOW_AT:
                        piece_low(i, *PIECE_LOW_AT[s])

            def a_alone(ia):
                a_rstd(ia)
                a_split(ia)

            a_alone(0)
            with pool.Fori(1, AHEAD) as ia:
                a_alone(ia)
            a_rstd(AHEAD)
            iteration(0, True, True)
            with pool.Fori(1, NIT - AHEAD - 1) as i:
                iteration(i, True, True)
            iteration(NIT - AHEAD - 1, True, False)
            with pool.Fori(NIT - AHEAD, NIT) as i:
                iteration(i, False, False)
            for s in range(POOL_LOW_LAG):
                low_step(NIT, s)

            def w2_split(n):
                pool.wait_ge(sem(f"w2_loaded{n}"), 16)
                pool.tensor_scalar(w2_piece(w2_h, n), w2_piece(w2_full, n), 1.0, 1.0, ALU.mult, ALU.mult)\
                    .then_inc(sem("w2_hi"), 1)
                pool.wait_ge(sem("w2_hi"), n + 1)
                low(w2_piece(w2_l, n), w2_piece(w2_full, n), w2_piece(w2_h, n)).then_inc(sem("w2_lo"), 1)

            def rstd_2(u):
                pool.wait_ge(sem("ln2_veps"), u + 1)
                pool.tensor_tensor(rstd2[:], veps2[:], power[:], ALU.pow).then_inc(sem("ln2_rstd"), 1)

            def hidden_low(u, m):
                pool.wait_ge(sem("h_hi"), u * FT + m + 1)
                low(h_l[:, m % 4, :], h_full[:, m % 4, :], h_h[:, m % 4, :]).then_inc(sem("h_lo"), 1)

            def rows(u, prepare):
                for m in range(FT):
                    hidden_low(u, m)
                    if prepare and m == RSTD_AT:
                        rstd_2(u + 1)

            for n in range(W2_PIECES // 2):
                w2_split(n)
            rstd_2(0)
            for n in range(W2_PIECES // 2, W2_PIECES):
                w2_split(n)
            rows(0, True)
            with pool.Fori(1, NA - 1) as u:
                rows(u, True)
            rows(NA - 1, False)


_INS = ['x', 'cond_1024', 'L0_cond_Wqkv', 'L0_cond_Wproj', 'L0_cond_bproj', 'L0_cond_W1', 'L0_cond_b1',
        'L0_cond_W2', 'L0_cond_b2', 'L0_cond_g1', 'L0_cond_be1', 'L0_cond_g2', 'L0_cond_be2', 'L0_cond_Wada',
        'L0_cond_bada']
_BY_PARTITION = ['L0_cond_b1', 'L0_cond_g1', 'L0_cond_be1', 'L0_cond_g2', 'L0_cond_be2']
_OUTS = [((8, 1024, 512), 'float32')]


def kernel(**inputs):
    import numpy as _np
    import concourse.bacc as _bacc
    from concourse import mybir as _mybir
    from concourse.bass_utils import run_bass_kernel_spmd as _run

    nc = _bacc.Bacc("TRN2", target_bir_lowering=False, num_devices=1)
    arrays, args = {}, []
    for name in _INS:
        a = _np.ascontiguousarray(inputs[name])
        if name in _BY_PARTITION:
            a = _np.ascontiguousarray(a.reshape(-1, P).T)
        arrays[f"in_{name}_dram"] = a
        args.append(nc.dram_tensor(f"in_{name}_dram", a.shape, _mybir.dt.from_np(a.dtype), kind="ExternalInput").ap())
    for i, (shape, dtype) in enumerate(_OUTS):
        dt = _mybir.dt.from_np(_np.dtype(dtype))
        args.append(nc.dram_tensor(f"out_{i}_dram", shape, dt, kind="ExternalOutput").ap())
    build(nc, *args)
    r = _run(nc, [arrays], core_ids=[0])
    got = tuple(r.results[0][f"out_{i}_dram"] for i in range(len(_OUTS)))
    return got[0]
```
